# Optimizing a Trainium2 kernel written in Bass

```python
import numpy as np
import jax
import jax.numpy as jnp

def _softmax(x, axis=-1):
    return jax.nn.softmax(x, axis=axis)

def _gelu(x):
    return jax.nn.gelu(x, approximate=True)

def _silu(x):
    return jax.nn.silu(x)

def _sigmoid(x):
    return jax.nn.sigmoid(x)

def _layernorm(x, axis=-1, eps=1e-05):
    m = jnp.mean(x, axis=axis, keepdims=True)
    v = jnp.var(x, axis=axis, keepdims=True)
    return (x - m) / jnp.sqrt(v + eps)

def _scatter_add(tgt, idx, src, axis=0):
    return tgt.at[idx].add(src)

def _segment_sum(src, seg, n):
    return jax.ops.segment_sum(src, seg, n)
kernel_name = 'mk_adj_preln_d4_adj_r2_be23f4'

def setup_inputs(seed: int=0):
    np.random.seed(seed)
    _w = jnp.asarray

    def _rec_inputs():
        import jax
        import jax.numpy as jnp
        _gk = jax.random.key(seed)
        x = -0.0005963 + 1.001 * jax.random.normal(jax.random.fold_in(_gk, 1), (16, 512, 384), jnp.float32)
        _a = jax.random.bernoulli(jax.random.fold_in(_gk, 2), 0.00390625, (16, 512, 512))
        _a = jnp.logical_or(_a, jnp.swapaxes(_a, -1, -2))
        _a = jnp.logical_or(_a, jnp.eye(512, dtype=bool))
        adj = _a
        return (x, adj)
    x, adj = _rec_inputs()

    def _L0_gnn_setup():
        import jax, jax.numpy as jnp
        import numpy as np
        ATT_HEAD = 12
        IN_DIM = 384
        OUT_DIM = IN_DIM // ATT_HEAD
        LEAKY_ALPHA = 0.2
        B, N = (8, 256)
        key = jax.random.key(seed)
        ks = jax.random.split(key, 8)
        feat_in = jax.random.normal(ks[0], (B, N, IN_DIM), dtype=jnp.float32)
        adj = jax.random.randint(ks[1], (B, N, N), 0, 2) > 0
        lim_W = float(np.sqrt(6.0 / (IN_DIM + OUT_DIM)))
        W = jax.random.uniform(ks[2], (ATT_HEAD, IN_DIM, OUT_DIM), minval=-lim_W, maxval=lim_W, dtype=jnp.float32)
        b = jnp.zeros((OUT_DIM,), dtype=jnp.float32)
        lim_w = float(np.sqrt(6.0 / (OUT_DIM + 1)))
        w_src = jax.random.uniform(ks[3], (ATT_HEAD, OUT_DIM, 1), minval=-lim_w, maxval=lim_w, dtype=jnp.float32)
        w_dst = jax.random.uniform(ks[4], (ATT_HEAD, OUT_DIM, 1), minval=-lim_w, maxval=lim_w, dtype=jnp.float32)
        std_H = float(np.sqrt(2.0 / (IN_DIM + IN_DIM)))
        H_w = jax.random.normal(ks[5], (IN_DIM, IN_DIM), dtype=jnp.float32) * std_H
        H_b = jax.random.normal(ks[6], (IN_DIM,), dtype=jnp.float32) * 0.01
        return {'feat_in': feat_in, 'adj': adj, 'W': W, 'b': b, 'w_src': w_src, 'w_dst': w_dst, 'H_w': H_w, 'H_b': H_b}
    _L0_gnn_all = _L0_gnn_setup()
    _L0_gnn_in = {k: v for k, v in _L0_gnn_all.items() if k in ('W', 'b', 'w_src', 'w_dst', 'H_w', 'H_b')}
    del _L0_gnn_all

    def _L1_gnn_setup():
        import jax, jax.numpy as jnp
        import numpy as np
        B, S, H = (4, 1024, 384)
        NUM_HEADS = 6
        HEAD_SIZE = H // NUM_HEADS
        NEG = -9000000000000000.0

        def _heads(x):
            b, s, _ = x.shape
            return x.reshape(b, s, NUM_HEADS, HEAD_SIZE).transpose(0, 2, 1, 3)
        key = jax.random.key(seed)
        ks = jax.random.split(key, 10)
        seq_inputs = jax.random.normal(ks[0], (B, S, H), dtype=jnp.float32)
        gm = jax.random.randint(ks[1], (B, S, S), 0, 2) > 0
        graph_mask = gm | jnp.eye(S, dtype=bool)[None]
        sc = 1.0 / np.sqrt(H)
        Wq = jax.random.normal(ks[2], (H, H), dtype=jnp.float32) * sc
        bq = jnp.zeros((H,), dtype=jnp.float32)
        Wk = jax.random.normal(ks[3], (H, H), dtype=jnp.float32) * sc
        bk = jnp.zeros((H,), dtype=jnp.float32)
        Wv = jax.random.normal(ks[4], (H, H), dtype=jnp.float32) * sc
        bv = jnp.zeros((H,), dtype=jnp.float32)
        Wf = jax.random.normal(ks[5], (H, H), dtype=jnp.float32) * sc
        bf = jnp.zeros((H,), dtype=jnp.float32)
        return {'seq_inputs': seq_inputs, 'Wq': Wq, 'bq': bq, 'Wk': Wk, 'bk': bk, 'Wv': Wv, 'bv': bv, 'Wf': Wf, 'bf': bf, 'graph_mask': graph_mask}
    _L1_gnn_all = _L1_gnn_setup()
    _L1_gnn_in = {k: v for k, v in _L1_gnn_all.items() if k in ('Wq', 'bq', 'Wk', 'bk', 'Wv', 'bv', 'Wf', 'bf')}
    del _L1_gnn_all

    def _L2_gnn_setup():
        import jax, jax.numpy as jnp
        import numpy as np
        ATT_HEAD = 12
        IN_DIM = 384
        OUT_DIM = IN_DIM // ATT_HEAD
        LEAKY_ALPHA = 0.2
        B, N = (8, 256)
        key = jax.random.key(seed)
        ks = jax.random.split(key, 8)
        feat_in = jax.random.normal(ks[0], (B, N, IN_DIM), dtype=jnp.float32)
        adj = jax.random.randint(ks[1], (B, N, N), 0, 2) > 0
        lim_W = float(np.sqrt(6.0 / (IN_DIM + OUT_DIM)))
        W = jax.random.uniform(ks[2], (ATT_HEAD, IN_DIM, OUT_DIM), minval=-lim_W, maxval=lim_W, dtype=jnp.float32)
        b = jnp.zeros((OUT_DIM,), dtype=jnp.float32)
        lim_w = float(np.sqrt(6.0 / (OUT_DIM + 1)))
        w_src = jax.random.uniform(ks[3], (ATT_HEAD, OUT_DIM, 1), minval=-lim_w, maxval=lim_w, dtype=jnp.float32)
        w_dst = jax.random.uniform(ks[4], (ATT_HEAD, OUT_DIM, 1), minval=-lim_w, maxval=lim_w, dtype=jnp.float32)
        std_H = float(np.sqrt(2.0 / (IN_DIM + IN_DIM)))
        H_w = jax.random.normal(ks[5], (IN_DIM, IN_DIM), dtype=jnp.float32) * std_H
        H_b = jax.random.normal(ks[6], (IN_DIM,), dtype=jnp.float32) * 0.01
        return {'feat_in': feat_in, 'adj': adj, 'W': W, 'b': b, 'w_src': w_src, 'w_dst': w_dst, 'H_w': H_w, 'H_b': H_b}
    _L2_gnn_all = _L2_gnn_setup()
    _L2_gnn_in = {k: v for k, v in _L2_gnn_all.items() if k in ('W', 'b', 'w_src', 'w_dst', 'H_w', 'H_b')}
    del _L2_gnn_all

    def _L3_gnn_setup():
        import jax, jax.numpy as jnp
        import numpy as np
        ATT_HEAD = 12
        IN_DIM = 384
        OUT_DIM = IN_DIM // ATT_HEAD
        LEAKY_ALPHA = 0.2
        B, N = (8, 256)
        key = jax.random.key(seed)
        ks = jax.random.split(key, 8)
        feat_in = jax.random.normal(ks[0], (B, N, IN_DIM), dtype=jnp.float32)
        adj = jax.random.randint(ks[1], (B, N, N), 0, 2) > 0
        lim_W = float(np.sqrt(6.0 / (IN_DIM + OUT_DIM)))
        W = jax.random.uniform(ks[2], (ATT_HEAD, IN_DIM, OUT_DIM), minval=-lim_W, maxval=lim_W, dtype=jnp.float32)
        b = jnp.zeros((OUT_DIM,), dtype=jnp.float32)
        lim_w = float(np.sqrt(6.0 / (OUT_DIM + 1)))
        w_src = jax.random.uniform(ks[3], (ATT_HEAD, OUT_DIM, 1), minval=-lim_w, maxval=lim_w, dtype=jnp.float32)
        w_dst = jax.random.uniform(ks[4], (ATT_HEAD, OUT_DIM, 1), minval=-lim_w, maxval=lim_w, dtype=jnp.float32)
        std_H = float(np.sqrt(2.0 / (IN_DIM + IN_DIM)))
        H_w = jax.random.normal(ks[5], (IN_DIM, IN_DIM), dtype=jnp.float32) * std_H
        H_b = jax.random.normal(ks[6], (IN_DIM,), dtype=jnp.float32) * 0.01
        return {'feat_in': feat_in, 'adj': adj, 'W': W, 'b': b, 'w_src': w_src, 'w_dst': w_dst, 'H_w': H_w, 'H_b': H_b}
    _L3_gnn_all = _L3_gnn_setup()
    _L3_gnn_in = {k: v for k, v in _L3_gnn_all.items() if k in ('W', 'b', 'w_src', 'w_dst', 'H_w', 'H_b')}
    del _L3_gnn_all
    return {'x': x, 'adj': adj, 'L0_gnn_W': _L0_gnn_in['W'], 'L0_gnn_b': _L0_gnn_in['b'], 'L0_gnn_w_src': _L0_gnn_in['w_src'], 'L0_gnn_w_dst': _L0_gnn_in['w_dst'], 'L0_gnn_H_w': _L0_gnn_in['H_w'], 'L0_gnn_H_b': _L0_gnn_in['H_b'], 'L1_gnn_Wq': _L1_gnn_in['Wq'], 'L1_gnn_bq': _L1_gnn_in['bq'], 'L1_gnn_Wk': _L1_gnn_in['Wk'], 'L1_gnn_bk': _L1_gnn_in['bk'], 'L1_gnn_Wv': _L1_gnn_in['Wv'], 'L1_gnn_bv': _L1_gnn_in['bv'], 'L1_gnn_Wf': _L1_gnn_in['Wf'], 'L1_gnn_bf': _L1_gnn_in['bf'], 'L2_gnn_W': _L2_gnn_in['W'], 'L2_gnn_b': _L2_gnn_in['b'], 'L2_gnn_w_src': _L2_gnn_in['w_src'], 'L2_gnn_w_dst': _L2_gnn_in['w_dst'], 'L2_gnn_H_w': _L2_gnn_in['H_w'], 'L2_gnn_H_b': _L2_gnn_in['H_b'], 'L3_gnn_W': _L3_gnn_in['W'], 'L3_gnn_b': _L3_gnn_in['b'], 'L3_gnn_w_src': _L3_gnn_in['w_src'], 'L3_gnn_w_dst': _L3_gnn_in['w_dst'], 'L3_gnn_H_w': _L3_gnn_in['H_w'], 'L3_gnn_H_b': _L3_gnn_in['H_b']}

def reference(x, adj, L0_gnn_W, L0_gnn_b, L0_gnn_w_src, L0_gnn_w_dst, L0_gnn_H_w, L0_gnn_H_b, L1_gnn_Wq, L1_gnn_bq, L1_gnn_Wk, L1_gnn_bk, L1_gnn_Wv, L1_gnn_bv, L1_gnn_Wf, L1_gnn_bf, L2_gnn_W, L2_gnn_b, L2_gnn_w_src, L2_gnn_w_dst, L2_gnn_H_w, L2_gnn_H_b, L3_gnn_W, L3_gnn_b, L3_gnn_w_src, L3_gnn_w_dst, L3_gnn_H_w, L3_gnn_H_b):
    import jax
    import jax.numpy as jnp

    def _L0_gnn_ref(feat_in, adj, W, b, w_src, w_dst, H_w, H_b):
        import jax, jax.numpy as jnp
        import numpy as np
        ATT_HEAD = 12
        IN_DIM = 384
        OUT_DIM = IN_DIM // ATT_HEAD
        LEAKY_ALPHA = 0.2
        B, N = (8, 256)
        h = jnp.einsum('bnd,ade->bane', feat_in, W)
        th = jnp.tanh(h)
        attn_src = jnp.einsum('bane,aeo->bano', th, w_src)
        attn_dst = jnp.einsum('bane,aeo->bano', th, w_dst)
        attn = attn_src + jnp.swapaxes(attn_dst, 2, 3)
        attn = jnp.where(attn >= 0, attn, LEAKY_ALPHA * attn)
        mask = ~adj[:, None, :, :]
        attn = jnp.where(mask, jnp.float32(-999.0), attn)
        attn = jax.nn.softmax(attn, axis=-1)
        feat_out = jnp.einsum('banm,bame->bane', attn, h) + b
        feat_out = jnp.swapaxes(feat_out, 1, 2).reshape(feat_in.shape[0], feat_in.shape[1], -1)
        feat_out = jax.nn.elu(feat_out)
        gate = jax.nn.sigmoid(feat_in @ H_w.T + H_b)
        return gate * feat_out + (1.0 - gate) * feat_in

    def _L1_gnn_ref(seq_inputs, Wq, bq, Wk, bk, Wv, bv, Wf, bf, graph_mask):
        import jax, jax.numpy as jnp
        import numpy as np
        B, S, H = (4, 1024, 384)
        NUM_HEADS = 6
        HEAD_SIZE = H // NUM_HEADS
        NEG = -9000000000000000.0

        def _heads(x):
            b, s, _ = x.shape
            return x.reshape(b, s, NUM_HEADS, HEAD_SIZE).transpose(0, 2, 1, 3)
        q = _heads(seq_inputs @ Wq + bq)
        k = _heads(seq_inputs @ Wk + bk)
        v = _heads(seq_inputs @ Wv + bv)
        scores = jnp.einsum('bhqd,bhkd->bhqk', q, k) / np.sqrt(HEAD_SIZE)
        bias = jnp.where(graph_mask, 0.0, NEG)[:, None]
        probs = jax.nn.softmax(scores + bias, axis=-1)
        ctx = jnp.einsum('bhqk,bhkd->bhqd', probs, v)
        ctx = ctx.transpose(0, 2, 1, 3).reshape(seq_inputs.shape[0], seq_inputs.shape[1], H)
        return ctx @ Wf + bf

    def _L2_gnn_ref(feat_in, adj, W, b, w_src, w_dst, H_w, H_b):
        import jax, jax.numpy as jnp
        import numpy as np
        ATT_HEAD = 12
        IN_DIM = 384
        OUT_DIM = IN_DIM // ATT_HEAD
        LEAKY_ALPHA = 0.2
        B, N = (8, 256)
        h = jnp.einsum('bnd,ade->bane', feat_in, W)
        th = jnp.tanh(h)
        attn_src = jnp.einsum('bane,aeo->bano', th, w_src)
        attn_dst = jnp.einsum('bane,aeo->bano', th, w_dst)
        attn = attn_src + jnp.swapaxes(attn_dst, 2, 3)
        attn = jnp.where(attn >= 0, attn, LEAKY_ALPHA * attn)
        mask = ~adj[:, None, :, :]
        attn = jnp.where(mask, jnp.float32(-999.0), attn)
        attn = jax.nn.softmax(attn, axis=-1)
        feat_out = jnp.einsum('banm,bame->bane', attn, h) + b
        feat_out = jnp.swapaxes(feat_out, 1, 2).reshape(feat_in.shape[0], feat_in.shape[1], -1)
        feat_out = jax.nn.elu(feat_out)
        gate = jax.nn.sigmoid(feat_in @ H_w.T + H_b)
        return gate * feat_out + (1.0 - gate) * feat_in

    def _L3_gnn_ref(feat_in, adj, W, b, w_src, w_dst, H_w, H_b):
        import jax, jax.numpy as jnp
        import numpy as np
        ATT_HEAD = 12
        IN_DIM = 384
        OUT_DIM = IN_DIM // ATT_HEAD
        LEAKY_ALPHA = 0.2
        B, N = (8, 256)
        h = jnp.einsum('bnd,ade->bane', feat_in, W)
        th = jnp.tanh(h)
        attn_src = jnp.einsum('bane,aeo->bano', th, w_src)
        attn_dst = jnp.einsum('bane,aeo->bano', th, w_dst)
        attn = attn_src + jnp.swapaxes(attn_dst, 2, 3)
        attn = jnp.where(attn >= 0, attn, LEAKY_ALPHA * attn)
        mask = ~adj[:, None, :, :]
        attn = jnp.where(mask, jnp.float32(-999.0), attn)
        attn = jax.nn.softmax(attn, axis=-1)
        feat_out = jnp.einsum('banm,bame->bane', attn, h) + b
        feat_out = jnp.swapaxes(feat_out, 1, 2).reshape(feat_in.shape[0], feat_in.shape[1], -1)
        feat_out = jax.nn.elu(feat_out)
        gate = jax.nn.sigmoid(feat_in @ H_w.T + H_b)
        return gate * feat_out + (1.0 - gate) * feat_in
    h = jnp.maximum(_layernorm(x, axis=-1), 0.0)
    x = x + _L0_gnn_ref(h, adj, L0_gnn_W, L0_gnn_b, L0_gnn_w_src, L0_gnn_w_dst, L0_gnn_H_w, L0_gnn_H_b)
    h = jnp.maximum(_layernorm(x, axis=-1), 0.0)
    x = x + _L1_gnn_ref(h, L1_gnn_Wq, L1_gnn_bq, L1_gnn_Wk, L1_gnn_bk, L1_gnn_Wv, L1_gnn_bv, L1_gnn_Wf, L1_gnn_bf, adj)
    h = jnp.maximum(_layernorm(x, axis=-1), 0.0)
    x = x + _L2_gnn_ref(h, adj, L2_gnn_W, L2_gnn_b, L2_gnn_w_src, L2_gnn_w_dst, L2_gnn_H_w, L2_gnn_H_b)
    h = jnp.maximum(_layernorm(x, axis=-1), 0.0)
    x = x + _L3_gnn_ref(h, adj, L3_gnn_W, L3_gnn_b, L3_gnn_w_src, L3_gnn_w_dst, L3_gnn_H_w, L3_gnn_H_b)
    return x

_drawn_inputs = setup_inputs


def setup_inputs(seed=0):
    import zlib

    import numpy as np

    out = dict(_drawn_inputs(seed))
    spreads = {'L0_gnn_b': (0.0, 0.1),
     'L1_gnn_bq': (0.0, 0.8),
     'L1_gnn_bk': (0.0, 2.0),
     'L1_gnn_bv': (0.0, 0.1),
     'L1_gnn_bf': (0.0, 0.1),
     'L2_gnn_b': (0.0, 0.498),
     'L3_gnn_b': (0.0, 0.491)}
    factors = {'L0_gnn_w_src': 10.246,
     'L0_gnn_H_b': 33.151,
     'L2_gnn_w_src': 15.95,
     'L2_gnn_H_b': 49.057,
     'L3_gnn_w_src': 18.034,
     'L3_gnn_H_b': 60.705}
    for name, (base, spread) in spreads.items():
        noise = np.random.default_rng([zlib.crc32(name.encode()), seed]).standard_normal(out[name].shape)
        drawn = base * np.exp(spread * noise) if base else spread * noise
        out[name] = jnp.asarray(drawn.astype(out[name].dtype))
    for name, factor in factors.items():
        out[name] = (out[name] * factor).astype(out[name].dtype)
    return out
```

```python
from contextlib import ExitStack

import concourse.bass as bass
from concourse import mybir

F32 = mybir.dt.float32
F32R = mybir.dt.float32r
BF16 = mybir.dt.bfloat16
U8 = mybir.dt.uint8
ALU = mybir.AluOpType
ACT = mybir.ActivationFunctionType
AX_X = mybir.AxisListType.X

P = 128
B = 16
N = 512
D = 384
NT = N // P
KC = D // P
H = 12
E = D // H
PAIRS = H // 2
MH = 6
MD = D // MH
EPS = 1e-5
NEG = -9000000000000000.0
Q0, Q1, Q2, Q3 = 0, 32, 64, 96

TASKS = 16
T_HNT, T_H = 0, 3
T_HT = (7, 9, 10)
T_Z = (8, 12, 13, 15)
T_SD, T_COL = 11, 14
SLOT_TASKS = ((0, 1, 2), (3, 4), (5, 6), (7, 8, 9, 10), (11, 12), (13, 14, 15))

UNITS = MH * NT
MPAIRS = MH // 2
MTASKS = 13
M_Q, M_K, M_V = 3, 6, 9
AT_PV = 11
AT_OUT = 5
AT_TASK = 10
CUT = 9


def program(nc, x, adj, adj_t, gat_w, gat_bias, gat_ws, wq, wk, wv, wf, mha_bias, mha_bf, out, passes=("g0", "m", "g2")):
    ctx = ExitStack()
    with ctx:
        def sb(name, shape, dt=F32):
            return ctx.enter_context(nc.sbuf_tensor(name, shape, dt))

        def sem(name):
            return ctx.enter_context(nc.semaphore(name))

        xin = sb("xin", [P, 2, NT, D])
        hn = sb("hn", [P, NT, D])
        hnT = sb("hnT", [P, KC, N])
        hn1 = sb("hn1", [P, NT, D])
        skip = sb("skip", [P, 2, NT, D])
        gate = sb("gate", [P, 2, NT, D])
        hb = sb("hb", [P, NT, D])
        thT = sb("thT", [P, KC, N])
        vals = sb("vals", [P, 2, NT, H, 64])
        ucol = sb("ucol", [P, 2, NT, H])
        dcol = sb("dcol", [P, NT, H])
        wts = sb("wts", [P, 2, 2, NT, N])
        accT = sb("accT", [P, 2, N])
        rcp = sb("rcp", [P, NT, 2])
        o1 = sb("o1", [P, 2, NT, D])
        ex = sb("ex", [P, NT, D])
        res = sb("res", [P, NT, D])
        rows = sb("rows", [P, N])
        rr = sb("rr", [H, N])
        vparts = sb("vparts", [P, 2, N], F32R)
        maskb = sb("maskb", [P, 2, NT, N], U8)
        wcat = sb("wcat", [P, KC, 2 * D])
        wcol = sb("wcol", [P, KC, 2])
        wsd = sb("wsd", [P, KC, 64])
        wts_row = wts[0:1, :, :, :, :].rearrange("p r a t n -> p (r a t n)")
        biasf = wts_row[:, 0:6 * D].rearrange("p (k d) -> p k d", k=3)
        biasp = wts_row[:, 6 * D:7 * D].bitcast(BF16).rearrange("p (k d) -> p k d", k=1)
        brow = sb("brow", [P, 2 * D], BF16)
        nb1 = sb("nb1", [P, 1])
        onesb = sb("onesb", [P, P], BF16)
        ident = sb("ident", [P, P])
        sel = sb("sel", [P, H, P], F32R)
        st6 = sb("st6", [P, NT, 6])
        mv = sb("mv", [P, NT, 2])
        veps = sb("veps", [P, NT])
        mhalf = sb("mhalf", [P, NT])
        minus1 = sb("minus1", [P, 1])
        rstd = sb("rstd", [P, NT])
        nmr = sb("nmr", [P, NT])
        dm = sb("dm", [P, 4])
        mwf = sb("mwf", [P, KC, D])
        negm = sb("negm", [P, 2, NT, N])
        mbias = sb("mbias", [P, 3, KC])
        nmax = sb("nmax", [P, 3])
        rsum = sb("rsum", [P, 3])
        rinv = sb("rinv", [P, 3])
        mwq, mwk = wcat[:, :, 0:D], wcat[:, :, D:2 * D]
        mwv = hb[:, 0:KC, :]
        kz = vals[:, :, :, :, :].rearrange("p s t a c -> p s (t a c)").rearrange("p s (h n) -> p s h n", h=MH)
        qT = gate[:, :, :, :].rearrange("p s t d -> p s (t d)").rearrange("p s (c n) -> p s c n", c=KC)
        mv_tile = skip
        probT = wts
        ctxT = thT
        scores = o1[:, 0, :, :].rearrange("p t d -> p (t d)").rearrange("p (r n) -> p r n", r=3)
        expd = ex[:, :, :].rearrange("p t d -> p (t d)").rearrange("p (r n) -> p r n", r=3)
        probs = hn1[:, :, :].rearrange("p t d -> p (t d)").rearrange("p (r n) -> p r n", r=3)
        banks = [ctx.enter_context(nc.psum_tensor(f"bank{i}", [P, 512], F32))[:, :] for i in range(8)]
        vbc, acc, back, ring = banks[0:4], banks[4], banks[5], banks[6:8]
        s_ps, pt_ps, ctx_ps, mring, out_ps = banks[0:2], banks[2:4], banks[4], banks[5:7], banks[7]

        x_in = [sem("x_in0"), sem("x_in1")]
        mask_in = [sem("mask_in0"), sem("mask_in1")]
        stored = sem("stored")
        w_in = sem("w_in")
        const_step = sem("const_step")
        waits_met = {e.engine: sem(n + "_waits_met") for n, e in (("dve", nc.vector), ("pool", nc.gpsimd), ("sp", nc.sync))}
        const_done = sem("const_done")
        wprep_pool = sem("wprep_pool")
        pool_const = sem("pool_const")
        bias_step = sem("bias_step")
        bias_done = sem("bias_done")
        bn_stats_done = sem("bn_stats_done")
        bn_aggr_done = sem("bn_aggr_done")
        var_ready = sem("var_ready")
        rstd_ready = sem("rstd_ready")
        nmr_ready = sem("nmr_ready")
        hn_ready = sem("hn_ready")
        xh_done = sem("xh_done")
        hn_used = sem("hn_used")
        gate_half = sem("gate_half")
        gate_prod = sem("gate_prod")
        gate_scaled = sem("gate_scaled")
        skip_ready = sem("skip_ready")
        task_done = sem("task_done")
        task_free = sem("task_free")
        dmax_done = sem("dmax_done")
        dmax_scaled = sem("dmax_scaled")
        dmax_ready = sem("dmax_ready")
        relu_sd = sem("relu_sd")
        rows_ready = sem("rows_ready")
        vhi_ready = sem("vhi_ready")
        vlo_ready = sem("vlo_ready")
        vals_ready = sem("vals_ready")
        vbc_done = sem("vbc_done")
        wts_ready = sem("wts_ready")
        acc_done = sem("acc_done")
        acc_free = sem("acc_free")
        back_done = sem("back_done")
        rcp_done = sem("rcp_done")
        o1_ready = sem("o1_ready")
        exp_done = sem("exp_done")
        elu_done = sem("elu_done")
        gated = sem("gated")
        res_ready = sem("res_ready")

        m_w_in = sem("m_w_in")
        m_bias_done = sem("m_bias_done")
        m_bias_step = sem("m_bias_step")
        m_stats_done = sem("m_stats_done")
        m_aggr_done = sem("m_aggr_done")
        m_var_ready = sem("m_var_ready")
        m_rstd_ready = sem("m_rstd_ready")
        m_nmr_ready = sem("m_nmr_ready")
        m_hn_ready = sem("m_hn_ready")
        m_task_done = sem("m_task_done")
        m_task_free = sem("m_task_free")
        m_negm_ready = sem("m_negm_ready")
        m_x_in = sem("m_x_in")
        m_score_done = sem("m_score_done")
        m_masked = sem("m_masked")
        m_exp_done = sem("m_exp_done")
        m_rinv_ready = sem("m_rinv_ready")
        m_prob_ready = sem("m_prob_ready")
        m_turned = sem("m_turned")
        m_probT_ready = sem("m_probT_ready")
        m_pv_done = sem("m_pv_done")
        m_ctx_ready = sem("m_ctx_ready")
        m_out_done = sem("m_out_done")
        m_out_read = sem("m_out_read")

        block = ctx.enter_context(nc.Block())

        def nodes(ap):
            return ap.rearrange("(t p) d -> p t d", p=P)

        def met(eng):
            eng.sem_inc(waits_met[eng.engine], 1)

        def earlier_pass(eng, graphs):
            if not isinstance(graphs, int) or graphs > 0:
                eng.wait_ge(stored, graphs * 16 + 1)

        def walk(eng, gat, mha):
            n = 0
            if "g0" in passes:
                gat(0, 0, x, 0)
                n += B
            if "m" in passes:
                mha(out if n else x, n)
                n += B
            if "g2" in passes:
                with eng.Fori(0, 2) as l:
                    gat(l * B + B, l + 1, out, n - B)

        def mha_units(eng, pre, at, drain):
            pre(0, 0)
            for u in range(CUT):
                at(0, 0, u, False, True)
            with eng.Fori(0, B // 2 - 1) as j:
                for s in range(2):
                    i = j * 2 + s
                    for u in range(CUT, UNITS):
                        at(i, s, u, True, True)
                    for u in range(CUT):
                        at(i + 1, 1 - s, u, True, True)
            for u in range(CUT, UNITS):
                at(B - 2, 0, u, True, True)
            for u in range(UNITS):
                at(B - 1, 1, u, True, False)
            drain(B - 1, 1)

        def gat_slots(eng, base, pre, slot, drain):
            pre(base, 0)
            slot(base, 0, 0, False, True)
            slot(base, 0, 1, False, True)
            slot(base, 0, 2, False, True)
            with eng.Fori(0, B // 2 - 1) as j:
                for s in range(2):
                    i = base + j * 2 + s
                    for p in range(3, PAIRS):
                        slot(i, s, p, True, True)
                    for p in range(3):
                        slot(i + 1, 1 - s, p, True, True)
            for p in range(3, PAIRS):
                slot(base + B - 2, 0, p, True, True)
            for p in range(PAIRS):
                slot(base + B - 1, 1, p, True, False)
            drain(base + B - 1, 1)

        @block.sync
        def _(sp):
            sp.sem_inc(stored, 1)

            def load_mask(s, src):
                sp.dma_start(maskb[:, s], src.rearrange("(t p) n -> p t n", p=P)).then_inc(mask_in[s], 16)

            def gat(base, layer, src, off):
                earlier_pass(sp, base + off)
                sp.dma_start(wcat[:, :, :], gat_w[layer].rearrange("(c p) n -> p c n", p=P)).then_inc(w_in, 16)
                sp.dma_start(wcol[:, :, :], gat_ws[layer].rearrange("(c p) s -> p c s", p=P)).then_inc(w_in, 16)
                sp.dma_start(biasf[:, 0, :], gat_bias[layer]).then_inc(w_in, 16)
                sp.dma_start(nb1[:, :], gat_bias[layer, 0, 0:P].rearrange("(p o) -> p o", o=1)).then_inc(w_in, 16)
                for s in range(2):
                    sp.dma_start(xin[:, s], nodes(src[s])).then_inc(x_in[s], 16)
                    load_mask(s, adj_t[s])

                def turn(i, k, s, more):
                    if more:
                        sp.wait_ge(skip_ready, i + 1)
                        met(sp)
                        sp.dma_start(xin[:, s], nodes(src[k + 2])).then_inc(x_in[s], 16)
                        sp.wait_ge(wts_ready, i * H + H)
                        met(sp)
                        load_mask(s, adj_t[k + 2])
                    sp.wait_ge(res_ready, i + 2)
                    met(sp)
                    sp.dma_start(nodes(out[k]), res[:, :, :]).then_inc(stored, 16)

                with sp.Fori(0, B // 2 - 1) as j:
                    for s in range(2):
                        turn(base + j * 2 + s, j * 2 + s, s, True)
                for s in range(2):
                    turn(base + B - 2 + s, B - 2 + s, s, False)

            def mha(src, before):
                earlier_pass(sp, before)
                for tile, w in ((mwq, wq), (mwk, wk), (mwv, wv), (mwf[:, :, :], wf)):
                    sp.dma_start(tile, w.rearrange("(c p) n -> p c n", p=P)).then_inc(m_w_in, 16)
                sp.dma_start(mbias[:, :, :], mha_bias).then_inc(m_w_in, 16)
                sp.dma_start(biasf[:, 0, 0:D], mha_bf).then_inc(m_w_in, 16)
                for s in range(2):
                    sp.dma_start(xin[:, s], nodes(src[s])).then_inc(x_in[s], 16)
                    load_mask(s, adj[s])
                sp.dma_start(res[:, :, :], nodes(src[0])).then_inc(m_x_in, 16)

                def turn(i, s, more):
                    if more:
                        sp.wait_ge(m_hn_ready, i + 1)
                        met(sp)
                        sp.dma_start(xin[:, s], nodes(src[i + 2])).then_inc(x_in[s], 16)
                        sp.wait_ge(m_negm_ready, i + 1)
                        met(sp)
                        load_mask(s, adj[i + 2])
                    sp.wait_ge(m_out_read, i * NT + NT + 1)
                    met(sp)
                    sp.dma_start(nodes(out[i]), res[:, :, :]).then_inc(stored, 16)

                def next_x(i):
                    sp.wait_ge(stored, (i + before) * 16 + 17)
                    met(sp)
                    sp.dma_start(res[:, :, :], nodes(src[i + 1])).then_inc(m_x_in, 16)

                with sp.Fori(0, B // 2 - 1) as j:
                    for s in range(2):
                        turn(j * 2 + s, s, True)
                        next_x(j * 2 + s)
                turn(B - 2, 0, False)
                next_x(B - 2)
                turn(B - 1, 1, False)

            walk(sp, gat, mha)
            total = {"g0": B, "g2": 2 * B, "m": B}
            sp.wait_ge(stored, 16 * sum(total[q] for q in passes) + 1)

        @block.tensor
        def _(pe):
            pe.wait_ge(const_done, 1)
            pe.sem_inc(back_done, 1)
            pe.sem_inc(m_pv_done, 1)
            pe.sem_inc(m_out_done, 1)

            def task(i, s, k):
                bank = ring[k % 2]
                if not (isinstance(i, int) and i == 0 and k < 2):
                    pe.wait_ge(task_free, i * TASKS + k - 1)
                if k < T_H:
                    if k == 0:
                        pe.wait_ge(hn_ready, i + 1)
                    for t in range(NT):
                        last = nc.tensor.transpose(bank[:, t * P:(t + 1) * P], hn[:, t, k * P:(k + 1) * P], ident[:, :])
                elif k < T_HT[0] or k in T_Z:
                    is_h = k < T_HT[0]
                    t = k - T_H if is_h else T_Z.index(k)
                    cols = slice(0, D) if is_h else slice(D, 2 * D)
                    if k == T_H:
                        pe.wait_ge(task_free, i * TASKS + T_H)
                    nc.tensor.matmul(bank[:, 0:D], onesb[:, :], brow[:, cols], start=True, stop=False)
                    for c in range(KC):
                        last = nc.tensor.matmul(bank[:, 0:D], hnT[:, c, t * P:(t + 1) * P], wcat[:, c, cols],
                                                start=False, stop=c == KC - 1)
                elif k in T_HT:
                    c = T_HT.index(k)
                    if c == 0:
                        pe.wait_ge(task_free, i * TASKS + k)
                    for t in range(NT):
                        last = nc.tensor.transpose(bank[:, t * P:(t + 1) * P], hb[:, t, c * P:(c + 1) * P], ident[:, :])
                elif k == T_SD:
                    pe.wait_ge(task_free, i * TASKS + T_SD)
                    for c in range(KC):
                        last = nc.tensor.matmul(bank[0:64, :], wsd[:, c, :], thT[:, c, :], start=c == 0, stop=c == KC - 1)
                else:
                    pe.wait_ge(rows_ready, i + 1)
                    for t in range(NT):
                        last = nc.tensor.transpose(bank[:, t * P:(t + 1) * P], rows[:, t * P:(t + 1) * P], ident[:, :])
                last.then_inc(task_done, 1)

            def broadcast_v(i, s, a):
                if a == 0:
                    pe.wait_ge(vlo_ready, i + 1)
                if not (isinstance(i, int) and i == 0 and a < 4):
                    pe.wait_ge(wts_ready, i * H + a - 3)
                nc.tensor.matmul(vbc[a % 4][:, :], sel[:, a, :], vparts[:, s, :], start=True, stop=True).then_inc(vbc_done, 1)

            def weighted_sums(i, s, p):
                pe.wait_ge(vals_ready, i + 1)
                pe.wait_ge(wts_ready, i * H + 2 * p + 2)
                if not (isinstance(i, int) and i == 0 and p < 1):
                    pe.wait_ge(acc_free, i * PAIRS + p + 1)
                for t in range(NT):
                    for a in range(2):
                        last = nc.tensor.matmul(acc[64 * a:64 * a + 64, :], vals[:, s, t, 2 * p + a, :],
                                                wts[:, p % 2, a, t, :], start=t == 0, stop=t == NT - 1,
                                                tile_position=(0, 64 * a))
                last.then_inc(acc_done, 1)

            def turn_back(i, p):
                pe.wait_ge(acc_free, i * PAIRS + p + 2)
                if not (isinstance(i, int) and i == 0 and p < 1):
                    pe.wait_ge(o1_ready, i * PAIRS + p + 1)
                for t in range(NT):
                    last = nc.tensor.transpose(back[:, t * P:(t + 1) * P], accT[:, p % 2, t * P:(t + 1) * P], ident[:, :])
                last.then_inc(back_done, 1)

            def gat(base, layer, src, off):
                pe.wait_ge(w_in, 64 * (layer + 1))
                pe.wait_ge(wprep_pool, layer + 1)
                pe.wait_ge(bias_done, layer + 1)

                def pre(i, s):
                    for k in range(TASKS):
                        task(i, s, k)
                    broadcast_v(i, s, 0)
                    broadcast_v(i, s, 1)

                def slot(i, s, p, prev, nxt):
                    if p >= 1:
                        weighted_sums(i, s, p - 1)
                    elif prev:
                        weighted_sums(i - 1, 1 - s, PAIRS - 1)
                    if p < PAIRS - 1:
                        broadcast_v(i, s, 2 * p + 2)
                        broadcast_v(i, s, 2 * p + 3)
                    for n, k in enumerate(SLOT_TASKS[p]):
                        if nxt:
                            task(i + 1, 1 - s, k)
                        if n == 0 and p >= 1:
                            turn_back(i, p - 1)
                        elif n == 0 and prev:
                            turn_back(i - 1, PAIRS - 1)
                    if p == PAIRS - 1 and nxt:
                        broadcast_v(i + 1, 1 - s, 0)
                        broadcast_v(i + 1, 1 - s, 1)

                def drain(i, s):
                    weighted_sums(i, s, PAIRS - 1)
                    turn_back(i, PAIRS - 1)

                gat_slots(pe, base, pre, slot, drain)

            def mha(src, before):
                pe.wait_ge(m_w_in, 16 * 6)
                pe.wait_ge(m_bias_done, 1)

                def mtask(i, s, k):
                    bank = mring[k % 2]
                    if not (isinstance(i, int) and i == 0 and k < 2):
                        pe.wait_ge(m_task_free, i * MTASKS + (k - 1 if k >= 2 else 0))
                    if k < M_Q:
                        if k == 0:
                            pe.wait_ge(m_hn_ready, i + 1)
                        for t in range(NT):
                            last = nc.tensor.transpose(bank[:, t * P:(t + 1) * P], hn[:, t, k * P:(k + 1) * P], ident[:, :])
                    elif k < M_V:
                        w, r = (mwq, k - M_Q) if k < M_K else (mwk, k - M_K)
                        if k == M_Q:
                            pe.wait_ge(m_task_free, i * MTASKS + M_Q)
                        for c in range(KC):
                            last = nc.tensor.matmul(bank[:, :], w[:, c, r * P:(r + 1) * P], hnT[:, c, :],
                                                    start=c == 0, stop=c == KC - 1)
                    else:
                        t = k - M_V
                        for c in range(KC):
                            last = nc.tensor.matmul(bank[:, 0:D], hnT[:, c, t * P:(t + 1) * P], mwv[:, c, :],
                                                    start=c == 0, stop=c == KC - 1)
                    last.then_inc(m_task_done, 1)

                def score(i, s, u):
                    h, t = u // NT, u % NT
                    if u == 0:
                        pe.wait_ge(m_task_free, i * MTASKS + M_V)
                    if not (isinstance(i, int) and i == 0 and u < 2):
                        pe.wait_ge(m_masked, i * UNITS + u - 1)
                    nc.tensor.matmul(s_ps[u % 2][:, :], qT[:, s, h // 2, t * P:(t + 1) * P], kz[:, s, h, :],
                                     start=True, stop=True).then_inc(m_score_done, 1)

                def turn_probs(i, u):
                    pe.wait_ge(m_prob_ready, i * UNITS + u + 1)
                    if not (isinstance(i, int) and i == 0 and u < 2):
                        pe.wait_ge(m_probT_ready, i * UNITS + u - 1)
                    for k in range(NT):
                        last = nc.tensor.transpose(pt_ps[u % 2][:, k * P:(k + 1) * P], probs[:, u % 3, k * P:(k + 1) * P], ident[:, :])
                    last.then_inc(m_turned, 1)

                def context(i, s, q):
                    pe.wait_ge(m_probT_ready, i * UNITS + 8 * q + 8)
                    pe.wait_ge(m_task_free, i * MTASKS + MTASKS)
                    pe.wait_ge(m_ctx_ready, i * MPAIRS + q + 1)
                    for k in range(NT):
                        for a in range(2):
                            h = 2 * q + a
                            last = nc.tensor.matmul(ctx_ps[64 * a:64 * a + 64, :], mv_tile[:, s, k, h * MD:(h + 1) * MD],
                                                    probT[:, (s + q) % 2, a, k, :], start=k == 0, stop=k == NT - 1,
                                                    tile_position=(0, 64 * a))
                    last.then_inc(m_pv_done, 1)

                def project(i, t):
                    if t == 0:
                        pe.wait_ge(m_ctx_ready, i * MPAIRS + MPAIRS + 1)
                    pe.wait_ge(m_out_read, i * NT + t + 1)
                    nc.tensor.matmul(out_ps[:, 0:D], onesb[:, :], brow[:, 0:D], start=True, stop=False)
                    for c in range(KC):
                        last = nc.tensor.matmul(out_ps[:, 0:D], ctxT[:, c, t * P:(t + 1) * P], mwf[:, c, :],
                                                start=False, stop=c == KC - 1)
                    last.then_inc(m_out_done, 1)

                def pre(i, s):
                    for k in range(MTASKS):
                        mtask(i, s, k)
                    score(i, s, 0)

                def at(i, s, u, prev, nxt):
                    if u < UNITS - 1:
                        score(i, s, u + 1)
                    elif nxt:
                        score(i + 1, 1 - s, 0)
                    if nxt and 0 <= u - AT_TASK < MTASKS:
                        mtask(i + 1, 1 - s, u - AT_TASK)
                    if prev and 0 <= u - AT_OUT < NT:
                        project(i - 1, u - AT_OUT)
                    if u >= 2:
                        turn_probs(i, u - 2)
                    elif prev:
                        turn_probs(i - 1, u - 2 + UNITS)
                    if u >= AT_PV and (u - AT_PV) % 8 == 0:
                        context(i, s, (u - AT_PV) // 8)
                    elif prev and (u + UNITS - AT_PV) // 8 == 2 and (u + UNITS - AT_PV) % 8 == 0:
                        context(i - 1, 1 - s, 2)

                def drain(i, s):
                    turn_probs(i, UNITS - 2)
                    turn_probs(i, UNITS - 1)
                    context(i, s, 2)
                    for t in range(NT):
                        project(i, t)

                mha_units(pe, pre, at, drain)

            walk(pe, gat, mha)

        @block.scalar
        def _(act):
            act.sem_inc(acc_free, 1)
            act.sem_inc(m_ctx_ready, 1)
            act.wait_ge(const_done, 1)

            def normalize(i, s):
                act.wait_ge(nmr_ready, i + 1)
                act.wait_ge(hn_used, i) if not (isinstance(i, int) and i == 0) else None
                for t in range(NT):
                    last = nc.scalar.activation(hn[:, t, :], xin[:, s, t, :], ACT.Relu, bias=nmr[:, t:t + 1], scale=rstd[:, t:t + 1])
                last.then_inc(hn_ready, 1)

            def empty(i, s, k):
                bank = ring[k % 2]
                act.wait_ge(task_done, i * TASKS + k + 1)
                if k < T_H:
                    last = nc.scalar.activation(hnT[:, k, :], bank[:, :], ACT.Copy)
                elif k < T_HT[0]:
                    if k == T_H and not (isinstance(i, int) and i == 0):
                        act.wait_ge(vals_ready, i)
                    last = nc.scalar.activation(hb[:, k - T_H, :], bank[:, 0:D], ACT.Copy)
                elif k in T_Z:
                    if k == T_Z[0] and not (isinstance(i, int) and i == 0):
                        act.wait_ge(res_ready, i)
                    last = nc.scalar.activation(gate[:, s, T_Z.index(k), :], bank[:, 0:D], ACT.Tanh, scale=0.5)
                elif k in T_HT:
                    last = nc.scalar.activation(thT[:, T_HT.index(k), :], bank[:, :], ACT.Tanh, bias=nb1[:, :])
                elif k == T_SD:
                    act.wait_ge(dmax_ready, i + 1)
                    nc.scalar.activation(rows[Q1:Q1 + H, :], bank[Q1:Q1 + H, :], ACT.Exp, bias=dm[Q1:Q1 + H, 1:2], scale=0.8)
                    nc.scalar.activation(rows[Q2:Q2 + H, :], bank[Q1:Q1 + H, :], ACT.Exp, bias=dm[Q1:Q1 + H, 2:3], scale=0.2)
                    last = nc.scalar.activation(rr[0:H, :], bank[0:H, :], ACT.Relu, bias=dm[0:H, 0:1])
                else:
                    nc.scalar.activation(ucol[:, s, :, :], bank.rearrange("p (t c) -> p t c", t=NT)[:, :, Q1:Q1 + H], ACT.Copy)
                    nc.scalar.activation(dcol[:, :, :], bank.rearrange("p (t c) -> p t c", t=NT)[:, :, Q2:Q2 + H], ACT.Copy)
                    last = nc.scalar.activation(vals[:, s, :, :, E], bank.rearrange("p (t c) -> p t c", t=NT)[:, :, Q2:Q2 + H], ACT.Copy)
                last.then_inc(task_free, 1)
                if k == T_SD:
                    act.wait_ge(task_free, i * TASKS + T_SD + 1)
                    nc.scalar.activation(rows[0:H, :], rr[0:H, :], ACT.Exp, scale=-0.8).then_inc(rows_ready, 1)
                    act.wait_ge(rows_ready, i + 1)
                    nc.scalar.activation(vparts[0:H, s, :], rows[0:H, :], ACT.Copy).then_inc(vhi_ready, 1)

            def copy_acc(i, p):
                act.wait_ge(acc_done, i * PAIRS + p + 1)
                if not (isinstance(i, int) and i == 0 and p < 2):
                    act.wait_ge(back_done, i * PAIRS + p)
                nc.scalar.activation(accT[:, p % 2, :], acc[:, :], ACT.Copy).then_inc(acc_free, 1)

            def exps(i, s):
                act.wait_ge(o1_ready, i * PAIRS + PAIRS + 1)
                if not (isinstance(i, int) and i == 0):
                    act.wait_ge(res_ready, i + 1)
                nc.scalar.activation(ex[:, :, :], o1[:, s, :, :], ACT.Exp, bias=minus1[:, :]).then_inc(exp_done, 1)

            def gat(base, layer, src, off):
                act.wait_ge(bias_done, layer + 1)

                def pre(i, s):
                    normalize(i, s)
                    for k in range(TASKS):
                        empty(i, s, k)

                def slot(i, s, p, prev, nxt):
                    if p == 2 and prev:
                        exps(i - 1, 1 - s)
                    if p >= 1:
                        copy_acc(i, p - 1)
                    elif prev:
                        copy_acc(i - 1, PAIRS - 1)
                    if nxt and p == 0:
                        normalize(i + 1, 1 - s)
                    if nxt:
                        for k in SLOT_TASKS[p]:
                            empty(i + 1, 1 - s, k)

                def drain(i, s):
                    copy_acc(i, PAIRS - 1)
                    exps(i, s)

                gat_slots(act, base, pre, slot, drain)

            def mha(src, before):
                act.wait_ge(m_bias_done, 1)

                def normalize(i, s):
                    act.wait_ge(m_nmr_ready, i + 1)
                    for t in range(NT):
                        last = nc.scalar.activation(hn[:, t, :], xin[:, s, t, :], ACT.Relu, bias=nmr[:, t:t + 1], scale=rstd[:, t:t + 1])
                    last.then_inc(m_hn_ready, 1)

                def empty(i, s, k):
                    bank = mring[k % 2]
                    act.wait_ge(m_task_done, i * MTASKS + k + 1)
                    if k < M_Q:
                        last = nc.scalar.activation(hnT[:, k, :], bank[:, :], ACT.Copy)
                    elif k < M_K:
                        last = nc.scalar.activation(qT[:, s, k - M_Q, :], bank[:, :], ACT.Identity,
                                                    bias=mbias[:, 0, k - M_Q:k - M_Q + 1], scale=0.125)
                    elif k < M_V:
                        c = k - M_K
                        for a in range(2):
                            half = slice(64 * a, 64 * a + 64)
                            last = nc.scalar.activation(kz[half, s, 2 * c + a, :], bank[half, :], ACT.Identity,
                                                        bias=mbias[half, 1, c:c + 1])
                    else:
                        last = nc.scalar.activation(mv_tile[:, s, k - M_V, :], bank[:, 0:D], ACT.Copy)
                    last.then_inc(m_task_free, 1)

                def exp(i, u):
                    act.wait_ge(m_masked, i * UNITS + u + 1)
                    if not (isinstance(i, int) and i == 0 and u < 3):
                        act.wait_ge(m_prob_ready, i * UNITS + u - 2)
                    r = u % 3
                    nc.scalar.activation(expd[:, r, :], scores[:, r, :], ACT.Exp, bias=nmax[:, r:r + 1], scale=-1.0,
                                         accum_out=rsum[:, r:r + 1]).then_inc(m_exp_done, 1)

                def copy_ctx(i, q):
                    act.wait_ge(m_pv_done, i * MPAIRS + q + 2)
                    if q == 0:
                        act.wait_ge(m_out_done, i * NT + 1)
                    nc.scalar.activation(ctxT[:, q, :], ctx_ps[:, :], ACT.Identity, bias=mbias[:, 2, q:q + 1]).then_inc(m_ctx_ready, 1)

                def pre(i, s):
                    normalize(i, s)
                    for k in range(MTASKS):
                        empty(i, s, k)

                def at(i, s, u, prev, nxt):
                    exp(i, u)
                    if nxt and u == AT_TASK - 1:
                        normalize(i + 1, 1 - s)
                    if nxt and 0 <= u - AT_TASK < MTASKS:
                        empty(i + 1, 1 - s, u - AT_TASK)
                    if u >= AT_PV and (u - AT_PV) % 8 == 0:
                        copy_ctx(i, (u - AT_PV) // 8)
                    elif prev and u == AT_PV + 16 - UNITS:
                        copy_ctx(i - 1, 2)

                mha_units(act, pre, at, lambda i, s: copy_ctx(i, 2))

            walk(act, gat, mha)

        @block.vector
        def _(dve):
            dve.sem_inc(o1_ready, 1)
            dve.sem_inc(res_ready, 1)
            dve.sem_inc(m_out_read, 1)
            nc.vector.memset(rows[:, :], 0.0)
            nc.vector.memset(vparts[:, :, :].bitcast(F32), 0.0)
            nc.vector.memset(brow[:, :], 0.0)
            nc.vector.memset(onesb[:, :], 0.0)
            nc.vector.memset(minus1[:, :], -1.0).then_inc(const_step, 1)
            dve.wait_ge(const_step, 1)
            for q in (Q0, Q1):
                nc.vector.memset(onesb[q:q + 1, :], 1.0)
            nc.vector.memset(onesb[Q2:Q2 + 1, :], 1.0).then_inc(const_step, 1)

            def ln_stats(s, loads, n, stats_done, aggr_done, var_done):
                dve.wait_ge(x_in[s], loads)
                for t in range(NT):
                    last = nc.vector.bn_stats(st6[:, t, :], xin[:, s, t, :])
                last.then_inc(stats_done, 1)
                dve.wait_ge(stats_done, n)
                met(dve)
                for t in range(NT):
                    last = nc.vector.bn_aggr(mv[:, t, :], st6[:, t, :])
                last.then_inc(aggr_done, 1)
                dve.wait_ge(aggr_done, n)
                nc.vector.tensor_scalar(veps[:, :], mv[:, :, 1], EPS, None, ALU.add).then_inc(var_done, 1)

            def bias_rows(layer):
                n = [layer * 6]

                def link(ins):
                    n[0] = n[0] + 1
                    ins.then_inc(bias_step, 1)
                    dve.wait_ge(bias_step, n[0])

                dve.wait_ge(w_in, 64 * (layer + 1))
                nc.vector.memset(vals[:, :, :, :, :], 0.0)
                nc.vector.tensor_scalar(nb1[:, :], nb1[:, :], -1.0, -1.0, ALU.mult, ALU.add)
                link(nc.vector.tensor_scalar(biasf[:, 0, 0:D], biasf[:, 0, 0:D], 1.0, None, ALU.add))
                link(nc.vector.tensor_copy(brow[0:1, :], biasf[:, 0, :]))
                link(nc.vector.tensor_tensor(biasf[:, 1, :], biasf[:, 0, :], brow[0:1, :], ALU.subtract))
                link(nc.vector.tensor_copy(biasp[:, 0, :], biasf[:, 1, :]))
                link(nc.vector.tensor_tensor(biasf[:, 2, :], biasf[:, 1, :], biasp[:, 0, :], ALU.subtract))
                link(nc.vector.tensor_copy(brow[Q1:Q1 + 1, :], biasp[:, 0, :]))
                nc.vector.tensor_copy(brow[Q2:Q2 + 1, :], biasf[:, 2, :]).then_inc(bias_done, 1)

            def neg_mean(i):
                dve.wait_ge(rstd_ready, i + 1)
                nc.vector.scalar_tensor_tensor(out=nmr[:, :], in0=mv[:, :, 0], scalar=-1.0, in1=rstd[:, :],
                                               op0=ALU.mult, op1=ALU.mult).then_inc(nmr_ready, 1)

            def dmax(i):
                sd = ring[T_SD % 2]
                dve.wait_ge(task_done, i * TASKS + T_SD + 1)
                nc.vector.tensor_reduce(dm[Q1:Q1 + H, 0:1], sd[Q1:Q1 + H, :], AX_X, ALU.max).then_inc(dmax_done, 1)
                dve.wait_ge(dmax_done, i + 1)
                nc.vector.tensor_scalar(dm[Q1:Q1 + H, 1:2], dm[Q1:Q1 + H, 0:1], -0.8, None, ALU.mult)
                nc.vector.tensor_scalar(dm[Q1:Q1 + H, 2:3], dm[Q1:Q1 + H, 0:1], -0.2, None, ALU.mult)
                nc.vector.tensor_copy(dm[0:H, 0:1], dm[Q1:Q1 + H, 0:1]).then_inc(dmax_ready, 1)

            def v_low(i, s):
                dve.wait_ge(vhi_ready, i + 1)
                nc.vector.tensor_tensor(vparts[Q1:Q1 + H, s, :], rows[0:H, :], vparts[0:H, s, :].bitcast(F32),
                                        ALU.subtract).then_inc(vlo_ready, 1)

            def values(i, s):
                dve.wait_ge(task_free, i * TASKS + T_COL + 1)
                nc.vector.tensor_tensor(vals[:, s, :, :, 0:E], hb[:, :, :].rearrange("p t (a e) -> p t a e", e=E),
                                        dcol[:, :, :].unsqueeze(3).to_broadcast([P, NT, H, E]),
                                        ALU.mult).then_inc(vals_ready, 1)

            def weights(i, s, a):
                dve.wait_ge(vbc_done, i * H + a + 1)
                if a % 2 == 0 and not (isinstance(i, int) and i == 0 and a < 4):
                    dve.wait_ge(acc_done, i * PAIRS + a // 2 - 1)
                for t in range(NT):
                    last = nc.vector.scalar_tensor_tensor(out=wts[:, a // 2 % 2, a % 2, t, :], in0=vbc[a % 4][:, :],
                                                          scalar=ucol[:, s, t, a:a + 1], in1=maskb[:, s, t, :],
                                                          op0=ALU.max, op1=ALU.mult)
                last.then_inc(wts_ready, 1)

            def divide(i, s, p):
                g = i * PAIRS + p + 1
                b4 = back.rearrange("p (t a c) -> p t a c", t=NT, a=2)
                dve.wait_ge(back_done, g + 1)
                nc.vector.reciprocal(rcp[:, :, :], b4[:, :, :, E]).then_inc(rcp_done, 1)
                dve.wait_ge(rcp_done, g)
                nc.vector.tensor_tensor(o1[:, s, :, 2 * p * E:(2 * p + 2) * E].rearrange("p t (a e) -> p t a e", e=E),
                                        b4[:, :, :, 0:E], rcp[:, :, :].unsqueeze(3).to_broadcast([P, NT, 2, E]),
                                        ALU.mult).then_inc(o1_ready, 1)

            def finish(i, s, off):
                dve.wait_ge(exp_done, i + 1)
                nc.vector.scalar_tensor_tensor(out=ex[:, :, :], in0=ex[:, :, :], scalar=1.0, in1=o1[:, s, :, :],
                                               op0=ALU.min, op1=ALU.max).then_inc(elu_done, 1)
                dve.wait_ge(elu_done, i + 1)
                dve.wait_ge(skip_ready, i + 1)
                nc.vector.tensor_tensor(ex[:, :, :], ex[:, :, :], gate[:, s, :, :], ALU.mult).then_inc(gated, 1)
                dve.wait_ge(gated, i + 1)
                dve.wait_ge(stored, (i + off) * 16 + 1)
                nc.vector.tensor_tensor(res[:, :, :], ex[:, :, :], skip[:, s, :, :], ALU.add).then_inc(res_ready, 1)

            def gat(base, layer, src, off):
                bias_rows(layer)

                def nth(i, s):
                    return 8 * (i + off - s) + 16

                def pre(i, s):
                    dve.wait_ge(mask_in[s], nth(i, s))
                    stats(i, s)
                    neg_mean(i)
                    dmax(i)
                    v_low(i, s)
                    values(i, s)

                def stats(i, s):
                    ln_stats(s, nth(i, s), i + 1, bn_stats_done, bn_aggr_done, var_ready)

                def slot(i, s, p, prev, nxt):
                    if p == 0 and prev:
                        dve.wait_ge(mask_in[s], nth(i, s))
                    if p == 0 and nxt:
                        stats(i + 1, 1 - s)
                    weights(i, s, 2 * p)
                    if p >= 2:
                        divide(i, s, p - 2)
                    elif prev:
                        divide(i - 1, 1 - s, PAIRS + p - 2)
                    if p == 0 and nxt:
                        neg_mean(i + 1)
                    if p == 5 and nxt:
                        v_low(i + 1, 1 - s)
                    weights(i, s, 2 * p + 1)
                    if p == 4 and nxt:
                        dmax(i + 1)
                    if p == 2 and prev:
                        finish(i - 1, 1 - s, off)
                    if p == 5 and nxt:
                        values(i + 1, 1 - s)

                def drain(i, s):
                    divide(i, s, PAIRS - 2)
                    divide(i, s, PAIRS - 1)
                    finish(i, s, off)

                gat_slots(dve, base, pre, slot, drain)

            def mha(src, before):
                dve.wait_ge(m_w_in, 16 * 6)
                made = [0]

                def link(ins):
                    made[0] += 1
                    ins.then_inc(m_bias_step, 1)
                    dve.wait_ge(m_bias_step, made[0])

                nc.vector.memset(kz, 0.0)
                nc.vector.tensor_scalar(mbias[:, 0, :], mbias[:, 0, :], 0.125, None, ALU.mult)
                link(nc.vector.tensor_copy(brow[0:1, 0:D], biasf[:, 0, 0:D]))
                link(nc.vector.tensor_tensor(biasf[:, 1, 0:D], biasf[:, 0, 0:D], brow[0:1, 0:D], ALU.subtract))
                link(nc.vector.tensor_copy(biasp[:, 0, 0:D], biasf[:, 1, 0:D]))
                link(nc.vector.tensor_tensor(biasf[:, 2, 0:D], biasf[:, 1, 0:D], biasp[:, 0, 0:D], ALU.subtract))
                link(nc.vector.tensor_copy(brow[Q1:Q1 + 1, 0:D], biasp[:, 0, 0:D]))
                nc.vector.tensor_copy(brow[Q2:Q2 + 1, 0:D], biasf[:, 2, 0:D]).then_inc(m_bias_done, 1)

                def stats(i, s):
                    ln_stats(s, 8 * (i + before - s) + 16, i + 1, m_stats_done, m_aggr_done, m_var_ready)

                def neg_mean(i):
                    dve.wait_ge(m_rstd_ready, i + 1)
                    nc.vector.scalar_tensor_tensor(out=nmr[:, :], in0=mv[:, :, 0], scalar=-1.0, in1=rstd[:, :],
                                                   op0=ALU.mult, op1=ALU.mult).then_inc(m_nmr_ready, 1)

                def masked(i, s, u):
                    if u == 0:
                        dve.wait_ge(m_negm_ready, i + 1)
                    dve.wait_ge(m_score_done, i * UNITS + u + 1)
                    if not (isinstance(i, int) and i == 0 and u < 3):
                        dve.wait_ge(m_exp_done, i * UNITS + u - 2)
                    met(dve)
                    r = u % 3
                    nc.vector.tensor_tensor_reduce(out=scores[:, r, :], in0=s_ps[u % 2][:, :], in1=negm[:, s, u % NT, :],
                                                   scale=-1.0, scalar=3e38, op0=ALU.add, op1=ALU.min,
                                                   accum_out=nmax[:, r:r + 1]).then_inc(m_masked, 1)

                def invert(i, u):
                    dve.wait_ge(m_exp_done, i * UNITS + u + 1)
                    if not (isinstance(i, int) and i == 0 and u < 3):
                        dve.wait_ge(m_prob_ready, i * UNITS + u - 2)
                    nc.vector.reciprocal(rinv[:, u % 3:u % 3 + 1], rsum[:, u % 3:u % 3 + 1]).then_inc(m_rinv_ready, 1)

                def copy_probT(i, s, u):
                    h, t = u // NT, u % NT
                    q = h // 2
                    dve.wait_ge(m_turned, i * UNITS + u + 1)
                    if u % 8 == 0 and not (isinstance(i, int) and i == 0 and q < 2):
                        dve.wait_ge(m_pv_done, i * MPAIRS + q)
                    nc.vector.tensor_copy(probT[:, (s + q) % 2, h % 2, :, t * P:(t + 1) * P],
                                          pt_ps[u % 2].rearrange("p (k n) -> p k n", k=NT)).then_inc(m_probT_ready, 1)

                def residual(i, t):
                    dve.wait_ge(m_out_done, i * NT + t + 2)
                    if t == 0:
                        dve.wait_ge(m_x_in, i * 16 + 16)
                    nc.vector.tensor_tensor(res[:, t, :], out_ps[:, 0:D], res[:, t, :], ALU.add).then_inc(m_out_read, 1)

                def pre(i, s):
                    dve.wait_ge(mask_in[s], 8 * (i + before - s) + 16)
                    stats(i, s)
                    neg_mean(i)

                def at(i, s, u, prev, nxt):
                    masked(i, s, u)
                    if nxt and u == AT_TASK - 3:
                        stats(i + 1, 1 - s)
                    if nxt and u == AT_TASK - 2:
                        neg_mean(i + 1)
                    if u >= 1:
                        invert(i, u - 1)
                    elif prev:
                        invert(i - 1, UNITS - 1)
                    if u >= 3:
                        copy_probT(i, s, u - 3)
                    elif prev:
                        copy_probT(i - 1, 1 - s, u - 3 + UNITS)
                    if prev and 0 <= u - AT_OUT < NT:
                        residual(i - 1, u - AT_OUT)

                def drain(i, s):
                    invert(i, UNITS - 1)
                    for u in range(UNITS - 3, UNITS):
                        copy_probT(i, s, u)
                    for t in range(NT):
                        residual(i, t)

                mha_units(dve, pre, at, drain)

            walk(dve, gat, mha)

        @block.gpsimd
        def _(pool):
            made = [0]

            def link(ins):
                made[0] += 1
                ins.then_inc(pool_const, 1)
                pool.wait_ge(pool_const, made[0])

            selF = ex[:, :, :].rearrange("p t (a c) -> p (t a) c", c=P)
            link(nc.gpsimd.memset(ident[:, :], 0.0))
            link(nc.gpsimd.memset(selF, 0.0))
            link(nc.gpsimd.memset(wsd[:, :, :], 0.0))
            link(nc.gpsimd.memset(mhalf[:, :], -0.5))
            link(nc.gpsimd.affine_select(out=ident[:, :], in_=ident[:, :], compare_op=ALU.not_equal, fill=1.0,
                                         base=0, pattern=[[-1, P]], channel_multiplier=1))
            for q in (Q0, Q1):
                link(nc.gpsimd.affine_select(out=selF, in_=selF, compare_op=ALU.not_equal, fill=1.0, base=-q,
                                             pattern=[[-1, H], [0, P]], channel_multiplier=1))
            link(nc.gpsimd.tensor_copy(sel[:, :, :], selF))
            pool.wait_ge(const_step, 2)
            pool.sem_inc(const_done, 1)

            def rsqrt(i):
                pool.wait_ge(var_ready, i + 1)
                nc.gpsimd.tensor_tensor(rstd[:, :], veps[:, :], mhalf[:, :], ALU.pow).then_inc(rstd_ready, 1)

            def skip_early(i, s):
                pool.wait_ge(hn_ready, i + 1)
                if not (isinstance(i, int) and i == 0):
                    pool.wait_ge(res_ready, i)
                nc.gpsimd.tensor_tensor(skip[:, s, :, :], xin[:, s, :, :], hn[:, :, :], ALU.add).then_inc(xh_done, 1)
                if not (isinstance(i, int) and i == 0):
                    pool.wait_ge(skip_ready, i)
                    met(pool)
                nc.gpsimd.tensor_scalar(hn1[:, :, :], hn[:, :, :], 1.0, 1.0, ALU.add, ALU.mult).then_inc(hn_used, 1)

            def skip_late(i, s):
                pool.wait_ge(task_free, i * TASKS + T_Z[-1] + 1)
                pool.wait_ge(hn_used, i + 1)
                met(pool)
                nc.gpsimd.tensor_scalar(gate[:, s, :, :], gate[:, s, :, :], 0.5, 0.5, ALU.mult, ALU.add).then_inc(gate_half, 1)
                pool.wait_ge(gate_half, i + 1)
                nc.gpsimd.tensor_tensor(hn1[:, :, :], hn1[:, :, :], gate[:, s, :, :], ALU.mult).then_inc(gate_prod, 1)
                pool.wait_ge(gate_prod, i + 1)
                pool.wait_ge(xh_done, i + 1)
                nc.gpsimd.tensor_tensor(skip[:, s, :, :], skip[:, s, :, :], hn1[:, :, :], ALU.subtract).then_inc(skip_ready, 1)

            def gat(base, layer, src, off):
                pool.wait_ge(w_in, 64 * (layer + 1))
                met(pool)
                for c in range(KC):
                    for j in range(4):
                        a = 4 * c + j
                        last = nc.gpsimd.tensor_copy(wsd[32 * j:32 * j + 32, c, a:a + 33:32], wcol[32 * j:32 * j + 32, c, :])
                last.then_inc(wprep_pool, 1)
                pool.wait_ge(wprep_pool, layer + 1)

                def pre(i, s):
                    rsqrt(i)
                    skip_early(i, s)

                def slot(i, s, p, prev, nxt):
                    if p == 0 and nxt:
                        rsqrt(i + 1)
                    if p == 0:
                        skip_late(i, s)
                    if p == 1 and nxt:
                        skip_early(i + 1, 1 - s)

                gat_slots(pool, base, pre, slot, lambda i, s: None)

            def mha(src, before):
                pool.wait_ge(m_w_in, 16 * 6)

                def rsqrt(i):
                    pool.wait_ge(m_var_ready, i + 1)
                    nc.gpsimd.tensor_tensor(rstd[:, :], veps[:, :], mhalf[:, :], ALU.pow).then_inc(m_rstd_ready, 1)

                def mask(i, s):
                    pool.wait_ge(mask_in[s], 8 * (i + before - s) + 16)
                    met(pool)
                    nc.gpsimd.tensor_scalar(negm[:, s, :, :], maskb[:, s, :, :], -1.0, -NEG, ALU.add, ALU.mult).then_inc(m_negm_ready, 1)

                def scale(i, u):
                    r = u % 3
                    pool.wait_ge(m_rinv_ready, i * UNITS + u + 1)
                    if not (isinstance(i, int) and i == 0 and u < 3):
                        pool.wait_ge(m_turned, i * UNITS + u - 2)
                    met(pool)
                    nc.gpsimd.tensor_scalar(probs[:, r, :], expd[:, r, :], rinv[:, r:r + 1], 1.0, ALU.mult, ALU.mult).then_inc(m_prob_ready, 1)

                def pre(i, s):
                    mask(i, s)
                    rsqrt(i)

                def at(i, s, u, prev, nxt):
                    if u >= 1:
                        scale(i, u - 1)
                    elif prev:
                        scale(i - 1, UNITS - 1)
                    if nxt and u == AT_TASK - 3:
                        rsqrt(i + 1)
                    if nxt and u == AT_TASK + 2:
                        mask(i + 1, 1 - s)

                mha_units(pool, pre, at, lambda i, s: scale(i, UNITS - 1))

            walk(pool, gat, mha)


def layout(inputs):
    import numpy as np

    def a(name):
        return np.asarray(inputs[name])

    gat = ("L0_gnn_", "L2_gnn_", "L3_gnn_")
    adj = a("adj")
    return {
        "x": np.ascontiguousarray(a("x")),
        "adj": np.ascontiguousarray(adj),
        "adj_t": np.ascontiguousarray(adj.transpose(0, 2, 1)),
        "gat_w": np.stack([np.concatenate([a(g + "W").transpose(1, 0, 2).reshape(D, D), a(g + "H_w").T], 1) for g in gat]),
        "gat_bias": np.stack([np.concatenate([np.tile(a(g + "b"), H), a(g + "H_b")])[None] for g in gat]),
        "gat_ws": np.stack([np.stack([a(g + "w_src").reshape(D), a(g + "w_dst").reshape(D)], 1) for g in gat]),
        "wq": a("L1_gnn_Wq"), "wk": a("L1_gnn_Wk"), "wv": a("L1_gnn_Wv"), "wf": a("L1_gnn_Wf"),
        "mha_bias": np.ascontiguousarray(np.stack([a("L1_gnn_" + n) for n in ("bq", "bk", "bv")]).reshape(3, KC, P).transpose(2, 0, 1)),
        "mha_bf": a("L1_gnn_bf")[None],
    }


def kernel(**inputs):
    import numpy as np
    import concourse.bacc as bacc
    from concourse import mybir as mb
    from concourse.bass_utils import run_bass_kernel_spmd

    arrays = layout(inputs)
    nc = bacc.Bacc("TRN2", target_bir_lowering=False, num_devices=1)
    aps = [nc.dram_tensor(n, v.shape, mb.dt.from_np(v.dtype), kind="ExternalInput").ap() for n, v in arrays.items()]
    out = nc.dram_tensor("out", (B, N, D), mb.dt.float32, kind="ExternalOutput").ap()
    program(nc, *aps, out)
    r = run_bass_kernel_spmd(nc, [arrays], core_ids=[0])
    return np.asarray(r.results[0]["out"])
```

```python
from contextlib import ExitStack

import concourse.bass as bass
from concourse import mybir

F32 = mybir.dt.float32
F32R = mybir.dt.float32r
BF16 = mybir.dt.bfloat16
U8 = mybir.dt.uint8
ALU = mybir.AluOpType
ACT = mybir.ActivationFunctionType
AX_X = mybir.AxisListType.X

P = 128
B = 16
N = 512
D = 384
NT = N // P
KC = D // P
H = 12
E = D // H
PAIRS = H // 2
MH = 6
MD = D // MH
EPS = 1e-5
NEG = -9000000000000000.0
Q0, Q1, Q2, Q3 = 0, 32, 64, 96

TASKS = 16
T_HNT, T_H = 0, 3
T_HT = (7, 9, 10)
T_Z = (8, 12, 13, 15)
T_SD, T_COL = 11, 14
SLOT_TASKS = ((0, 1, 2), (3, 4), (5, 6), (7, 8, 9, 10), (11, 12), (13, 14, 15))

UNITS = MH * NT
MPAIRS = MH // 2
MTASKS = (("hT", 0), ("hT", 1), ("hT", 2), ("q", 0), ("v", 0), ("k", 0), ("v", 1), ("q", 1), ("v", 2),
          ("k", 1), ("v", 3), ("q", 2), ("k", 2))
MT = len(MTASKS)
SPLIT = tuple(n for n, (kind, c) in enumerate(MTASKS) if kind in "qk")
TASK_AT = {10: 0, 11: 1, 12: 2, 13: 3, 14: 4, 16: 5, 17: 6, 19: 7, 21: 8, 22: 9}
LATE_AT = {0: 10, 1: 11, 3: 12}
AT_STATS = 5
TURN = 3
AT_PV = 9 + TURN
OUT_AT = {6: 0, 7: 1, 8: 2, 10: 3}
CUT = 11


def program(nc, x, adj, adj_t, gat_w, gat_bias, gat_ws, wq, wk, wv, wf, mha_bias, mha_bf, out, passes=("g0", "m", "g2")):
    ctx = ExitStack()
    with ctx:
        def sb(name, shape, dt=F32):
            return ctx.enter_context(nc.sbuf_tensor(name, shape, dt))

        def sem(name):
            return ctx.enter_context(nc.semaphore(name))

        xin = sb("xin", [P, 2, NT, D])
        hn = sb("hn", [P, NT, D])
        hnT = sb("hnT", [P, KC, N])
        hn1 = sb("hn1", [P, NT, D])
        skip = sb("skip", [P, 2, NT, D])
        with nc.sbuf_tensor("gate", [P, 2, NT, D], F32) as gate:
            pass
        q_parts = sb("q_parts", [P, MH, N], F32R)
        with nc.sbuf_tensor("vals", [P, 2, NT, H, 64], F32) as vals:
            pass
        k_parts = sb("k_parts", [P, 2, MH, N], F32R)
        hb = sb("hb", [P, NT, D])
        thT = sb("thT", [P, KC, N])
        ucol = sb("ucol", [P, 2, NT, H])
        dcol = sb("dcol", [P, NT, H])
        wts = sb("wts", [P, 2, 2, NT, N])
        accT = sb("accT", [P, 2, N])
        rcp = sb("rcp", [P, NT, 2])
        o1 = sb("o1", [P, 2, NT, D])
        ex = sb("ex", [P, NT, D])
        res = sb("res", [P, NT, D])
        rows = sb("rows", [P, N])
        rr = sb("rr", [H, N])
        vparts = sb("vparts", [P, 2, N], F32R)
        maskb = sb("maskb", [P, 2, NT, N], U8)
        wcat = sb("wcat", [P, KC, 2 * D])
        wcol = sb("wcol", [P, KC, 2])
        wsd = sb("wsd", [P, KC, 64])
        wts_row = wts[0:1, :, :, :, :].rearrange("p r a t n -> p (r a t n)")
        biasf = wts_row[:, 0:6 * D].rearrange("p (k d) -> p k d", k=3)
        biasp = wts_row[:, 6 * D:7 * D].bitcast(BF16).rearrange("p (k d) -> p k d", k=1)
        brow = sb("brow", [P, 2 * D], BF16)
        nb1 = sb("nb1", [P, 1])
        onesb = sb("onesb", [P, P], BF16)
        ident = sb("ident", [P, P])
        sel = sb("sel", [P, H, P], F32R)
        st6 = sb("st6", [P, NT, 6])
        mv = sb("mv", [P, NT, 2])
        veps = sb("veps", [P, NT])
        mhalf = sb("mhalf", [P, NT])
        minus1 = sb("minus1", [P, 1])
        rstd = sb("rstd", [P, NT])
        nmr = sb("nmr", [P, NT])
        dm = sb("dm", [P, 4])
        mwf = sb("mwf", [P, KC, D])
        negm = sb("negm", [P, 2, NT, N])
        mbias = sb("mbias", [P, 3, KC])
        nmax = sb("nmax", [P, 3])
        rsum = sb("rsum", [P, 3])
        rinv = sb("rinv", [P, 3])
        mwq, mwk = wcat[:, :, 0:D], wcat[:, :, D:2 * D]
        mwv = hb[:, 0:KC, :]
        mv_tile = skip
        probT = wts
        ctxT = thT
        scores = o1[:, 0, :, :].rearrange("p t d -> p (t d)").rearrange("p (r n) -> p r n", r=3)
        expd = ex[:, :, :].rearrange("p t d -> p (t d)").rearrange("p (r n) -> p r n", r=3)
        probs = hn1[:, :, :].rearrange("p t d -> p (t d)").rearrange("p (r n) -> p r n", r=3)
        selF = ex[:, :, :].rearrange("p t (a c) -> p (t a) c", c=P)
        banks = [ctx.enter_context(nc.psum_tensor(f"bank{i}", [P, 512], F32))[:, :] for i in range(8)]
        vbc, acc, back, ring = banks[0:4], banks[4], banks[5], banks[6:8]
        s_ps, pt_ps, ctx_ps, mring, out_ps = banks[0:2], banks[2:4], banks[4], banks[5:7], banks[7]

        x_in = [sem("x_in0"), sem("x_in1")]
        mask_in = [sem("mask_in0"), sem("mask_in1")]
        stored = sem("stored")
        w_in = sem("w_in")
        const_step = sem("const_step")
        waits_met = {e.engine: sem(n + "_waits_met") for n, e in (("dve", nc.vector), ("pool", nc.gpsimd), ("sp", nc.sync))}
        const_done = sem("const_done")
        sel_ready = sem("sel_ready")
        wprep_pool = sem("wprep_pool")
        pool_const = sem("pool_const")
        bias_step = sem("bias_step")
        bias_done = sem("bias_done")
        bn_stats_done = sem("bn_stats_done")
        bn_aggr_done = sem("bn_aggr_done")
        var_ready = sem("var_ready")
        rstd_ready = sem("rstd_ready")
        nmr_ready = sem("nmr_ready")
        hn_ready = sem("hn_ready")
        xh_done = sem("xh_done")
        hn_used = sem("hn_used")
        gate_half = sem("gate_half")
        gate_prod = sem("gate_prod")
        gate_scaled = sem("gate_scaled")
        skip_ready = sem("skip_ready")
        task_done = sem("task_done")
        task_free = sem("task_free")
        dmax_done = sem("dmax_done")
        dmax_scaled = sem("dmax_scaled")
        dmax_ready = sem("dmax_ready")
        relu_sd = sem("relu_sd")
        rows_ready = sem("rows_ready")
        vhi_ready = sem("vhi_ready")
        vlo_ready = sem("vlo_ready")
        vals_cleared = sem("vals_cleared")
        vals_ready = sem("vals_ready")
        vbc_done = sem("vbc_done")
        wts_ready = sem("wts_ready")
        acc_done = sem("acc_done")
        acc_free = sem("acc_free")
        back_done = sem("back_done")
        rcp_done = sem("rcp_done")
        o1_ready = sem("o1_ready")
        exp_done = sem("exp_done")
        elu_done = sem("elu_done")
        gated = sem("gated")
        res_ready = sem("res_ready")

        m_w_in = sem("m_w_in")
        m_bias_done = sem("m_bias_done")
        m_bias_step = sem("m_bias_step")
        m_stats_done = sem("m_stats_done")
        m_aggr_done = sem("m_aggr_done")
        m_var_ready = sem("m_var_ready")
        m_rstd_ready = sem("m_rstd_ready")
        m_nmr_ready = sem("m_nmr_ready")
        m_hn_ready = sem("m_hn_ready")
        m_task_done = sem("m_task_done")
        m_task_free = sem("m_task_free")
        m_split = sem("m_split")
        m_k_doubled = sem("m_k_doubled")
        m_negm_ready = sem("m_negm_ready")
        m_x_in = sem("m_x_in")
        m_score_done = sem("m_score_done")
        m_masked = sem("m_masked")
        m_exp_done = sem("m_exp_done")
        m_rinv_ready = sem("m_rinv_ready")
        m_prob_ready = sem("m_prob_ready")
        m_turned = sem("m_turned")
        m_probT_ready = sem("m_probT_ready")
        m_pv_done = sem("m_pv_done")
        m_ctx_ready = sem("m_ctx_ready")
        m_out_done = sem("m_out_done")
        m_out_read = sem("m_out_read")

        block = ctx.enter_context(nc.Block())

        def nodes(ap):
            return ap.rearrange("(t p) d -> p t d", p=P)

        def met(eng):
            eng.sem_inc(waits_met[eng.engine], 1)

        def earlier_pass(eng, graphs):
            if not isinstance(graphs, int) or graphs > 0:
                eng.wait_ge(stored, graphs * 16 + 1)

        def walk(eng, gat, mha):
            n = 0
            if "g0" in passes:
                gat(0, 0, x, 0)
                n += B
            if "m" in passes:
                mha(out if n else x, n)
                n += B
            if "g2" in passes:
                with eng.Fori(0, 2) as l:
                    gat(l * B + B, l + 1, out, n - B)

        def mha_units(eng, pre, at, drain):
            pre(0, 0)
            for u in range(CUT):
                at(0, 0, u, False, True)
            with eng.Fori(0, B // 2 - 1) as j:
                for s in range(2):
                    i = j * 2 + s
                    for u in range(CUT, UNITS):
                        at(i, s, u, True, True)
                    for u in range(CUT):
                        at(i + 1, 1 - s, u, True, True)
            for u in range(CUT, UNITS):
                at(B - 2, 0, u, True, True)
            for u in range(UNITS):
                at(B - 1, 1, u, True, False)
            drain(B - 1, 1)

        def gat_slots(eng, base, pre, slot, drain):
            pre(base, 0)
            for p in range(3):
                slot(base, 0, p, False, 2)
            with eng.Fori(0, B // 2 - 1) as j:
                for s in range(2):
                    i = base + j * 2 + s
                    for p in range(3, PAIRS):
                        slot(i, s, p, True, 2)
                    for p in range(3):
                        slot(i + 1, 1 - s, p, True, 2)
            for p in range(3, PAIRS):
                slot(base + B - 2, 0, p, True, 1)
            for p in range(PAIRS):
                slot(base + B - 1, 1, p, True, 0)
            drain(base + B - 1, 1)

        @block.sync
        def _(sp):
            sp.sem_inc(stored, 1)

            def load_mask(s, src):
                sp.dma_start(maskb[:, s], src.rearrange("(t p) n -> p t n", p=P)).then_inc(mask_in[s], 16)

            def gat(base, layer, src, off):
                earlier_pass(sp, base + off)
                sp.dma_start(xin[:, 0], nodes(src[0])).then_inc(x_in[0], 16)
                sp.dma_start(wcat[:, :, :], gat_w[layer].rearrange("(c p) n -> p c n", p=P)).then_inc(w_in, 16)
                sp.dma_start(wcol[:, :, :], gat_ws[layer].rearrange("(c p) s -> p c s", p=P)).then_inc(w_in, 16)
                sp.dma_start(biasf[:, 0, :], gat_bias[layer]).then_inc(w_in, 16)
                sp.dma_start(nb1[:, :], gat_bias[layer, 0, 0:P].rearrange("(p o) -> p o", o=1)).then_inc(w_in, 16)
                load_mask(0, adj_t[0])
                sp.dma_start(xin[:, 1], nodes(src[1])).then_inc(x_in[1], 16)
                load_mask(1, adj_t[1])

                def turn(i, k, s, more):
                    if more:
                        sp.wait_ge(skip_ready, i + 1)
                        met(sp)
                        sp.dma_start(xin[:, s], nodes(src[k + 2])).then_inc(x_in[s], 16)
                        sp.wait_ge(wts_ready, i * H + H)
                        met(sp)
                        load_mask(s, adj_t[k + 2])
                    sp.wait_ge(res_ready, i + 2)
                    met(sp)
                    sp.dma_start(nodes(out[k]), res[:, :, :]).then_inc(stored, 16)

                with sp.Fori(0, B // 2 - 1) as j:
                    for s in range(2):
                        turn(base + j * 2 + s, j * 2 + s, s, True)
                for s in range(2):
                    turn(base + B - 2 + s, B - 2 + s, s, False)

            def mha(src, before):
                earlier_pass(sp, before)
                for tile, w in ((mwq, wq), (mwk, wk), (mwv, wv), (mwf[:, :, :], wf)):
                    sp.dma_start(tile, w.rearrange("(c p) n -> p c n", p=P)).then_inc(m_w_in, 16)
                sp.dma_start(mbias[:, :, :], mha_bias).then_inc(m_w_in, 16)
                sp.dma_start(biasf[:, 0, 0:D], mha_bf).then_inc(m_w_in, 16)
                for s in range(2):
                    sp.dma_start(xin[:, s], nodes(src[s])).then_inc(x_in[s], 16)
                    load_mask(s, adj[s])
                sp.dma_start(res[:, :, :], nodes(src[0])).then_inc(m_x_in, 16)

                def turn(i, s, more):
                    if more:
                        sp.wait_ge(m_hn_ready, i + 1)
                        met(sp)
                        sp.dma_start(xin[:, s], nodes(src[i + 2])).then_inc(x_in[s], 16)
                        sp.wait_ge(m_negm_ready, i + 1)
                        met(sp)
                        load_mask(s, adj[i + 2])
                    sp.wait_ge(m_out_read, i * NT + NT + 1)
                    met(sp)
                    sp.dma_start(nodes(out[i]), res[:, :, :]).then_inc(stored, 16)

                def next_x(i):
                    sp.wait_ge(stored, (i + before) * 16 + 17)
                    met(sp)
                    sp.dma_start(res[:, :, :], nodes(src[i + 1])).then_inc(m_x_in, 16)

                with sp.Fori(0, B // 2 - 1) as j:
                    for s in range(2):
                        turn(j * 2 + s, s, True)
                        next_x(j * 2 + s)
                turn(B - 2, 0, False)
                next_x(B - 2)
                turn(B - 1, 1, False)

            walk(sp, gat, mha)
            total = {"g0": B, "g2": 2 * B, "m": B}
            sp.wait_ge(stored, 16 * sum(total[q] for q in passes) + 1)

        @block.tensor
        def _(pe):
            pe.wait_ge(const_done, 1)
            pe.wait_ge(sel_ready, 1)
            pe.sem_inc(back_done, 1)
            pe.sem_inc(m_pv_done, 1)
            pe.sem_inc(m_out_done, 1)

            def task(i, s, k):
                bank = ring[k % 2]
                if not (isinstance(i, int) and i == 0 and k < 2):
                    pe.wait_ge(task_free, i * TASKS + k - 1)
                if k < T_H:
                    if k == 0:
                        pe.wait_ge(hn_ready, i + 1)
                    for t in range(NT):
                        last = nc.tensor.transpose(bank[:, t * P:(t + 1) * P], hn[:, t, k * P:(k + 1) * P], ident[:, :])
                elif k < T_HT[0] or k in T_Z:
                    is_h = k < T_HT[0]
                    t = k - T_H if is_h else T_Z.index(k)
                    cols = slice(0, D) if is_h else slice(D, 2 * D)
                    if k == T_H:
                        pe.wait_ge(task_free, i * TASKS + T_H)
                    nc.tensor.matmul(bank[:, 0:D], onesb[:, :], brow[:, cols], start=True, stop=False)
                    for c in range(KC):
                        last = nc.tensor.matmul(bank[:, 0:D], hnT[:, c, t * P:(t + 1) * P], wcat[:, c, cols],
                                                start=False, stop=c == KC - 1)
                elif k in T_HT:
                    c = T_HT.index(k)
                    if c == 0:
                        pe.wait_ge(task_free, i * TASKS + k)
                    for t in range(NT):
                        last = nc.tensor.transpose(bank[:, t * P:(t + 1) * P], hb[:, t, c * P:(c + 1) * P], ident[:, :])
                elif k == T_SD:
                    pe.wait_ge(task_free, i * TASKS + T_SD)
                    for c in range(KC):
                        last = nc.tensor.matmul(bank[0:64, :], wsd[:, c, :], thT[:, c, :], start=c == 0, stop=c == KC - 1)
                else:
                    pe.wait_ge(rows_ready, i + 1)
                    for t in range(NT):
                        last = nc.tensor.transpose(bank[:, t * P:(t + 1) * P], rows[:, t * P:(t + 1) * P], ident[:, :])
                last.then_inc(task_done, 1)

            def broadcast_v(i, s, a):
                if a == 0:
                    pe.wait_ge(vlo_ready, i + 1)
                if not (isinstance(i, int) and i == 0 and a < 4):
                    pe.wait_ge(wts_ready, i * H + a - 3)
                nc.tensor.matmul(vbc[a % 4][:, :], sel[:, a, :], vparts[:, s, :], start=True, stop=True).then_inc(vbc_done, 1)

            def weighted_sums(i, s, p):
                pe.wait_ge(vals_ready, i + 1)
                pe.wait_ge(wts_ready, i * H + 2 * p + 2)
                if not (isinstance(i, int) and i == 0 and p < 1):
                    pe.wait_ge(acc_free, i * PAIRS + p + 1)
                for t in range(NT):
                    for a in range(2):
                        last = nc.tensor.matmul(acc[64 * a:64 * a + 64, :], vals[:, s, t, 2 * p + a, :],
                                                wts[:, p % 2, a, t, :], start=t == 0, stop=t == NT - 1,
                                                tile_position=(0, 64 * a))
                last.then_inc(acc_done, 1)

            def turn_back(i, p):
                pe.wait_ge(acc_free, i * PAIRS + p + 2)
                if not (isinstance(i, int) and i == 0 and p < 1):
                    pe.wait_ge(o1_ready, i * PAIRS + p + 1)
                for t in range(NT):
                    last = nc.tensor.transpose(back[:, t * P:(t + 1) * P], accT[:, p % 2, t * P:(t + 1) * P], ident[:, :])
                last.then_inc(back_done, 1)

            def gat(base, layer, src, off):
                def pre(i, s):
                    for k in range(TASKS):
                        if k == T_H:
                            pe.wait_ge(w_in, 64 * (layer + 1))
                            pe.wait_ge(bias_done, layer + 1)
                        if k == T_SD:
                            pe.wait_ge(wprep_pool, layer + 1)
                        task(i, s, k)
                    broadcast_v(i, s, 0)
                    broadcast_v(i, s, 1)

                def slot(i, s, p, prev, nxt):
                    if p >= 1:
                        weighted_sums(i, s, p - 1)
                    elif prev:
                        weighted_sums(i - 1, 1 - s, PAIRS - 1)
                    if p < PAIRS - 1:
                        broadcast_v(i, s, 2 * p + 2)
                        broadcast_v(i, s, 2 * p + 3)
                    for n, k in enumerate(SLOT_TASKS[p]):
                        if nxt:
                            task(i + 1, 1 - s, k)
                        if n == 0 and p >= 1:
                            turn_back(i, p - 1)
                        elif n == 0 and prev:
                            turn_back(i - 1, PAIRS - 1)
                    if p == PAIRS - 1 and nxt:
                        broadcast_v(i + 1, 1 - s, 0)
                        broadcast_v(i + 1, 1 - s, 1)

                def drain(i, s):
                    weighted_sums(i, s, PAIRS - 1)
                    turn_back(i, PAIRS - 1)

                gat_slots(pe, base, pre, slot, drain)

            def mha(src, before):
                pe.wait_ge(m_w_in, 16 * 6)
                pe.wait_ge(m_bias_done, 1)

                def mtask(i, s, n):
                    kind, c = MTASKS[n]
                    bank = mring[n % 2]
                    if not (isinstance(i, int) and i == 0 and n < 2):
                        pe.wait_ge(m_task_free, i * MT + (n - 1 if n >= 2 else 0))
                        if n < 2:
                            pe.wait_ge(m_split, i * len(SPLIT))
                        elif n - 2 in SPLIT:
                            pe.wait_ge(m_split, i * len(SPLIT) + SPLIT.index(n - 2) + 1)
                    if kind == "hT":
                        if c == 0:
                            pe.wait_ge(m_hn_ready, i + 1)
                        for t in range(NT):
                            last = nc.tensor.transpose(bank[:, t * P:(t + 1) * P], hn[:, t, c * P:(c + 1) * P], ident[:, :])
                    elif kind == "v":
                        for k in range(KC):
                            last = nc.tensor.matmul(bank[:, 0:D], hnT[:, k, c * P:(c + 1) * P], mwv[:, k, :],
                                                    start=k == 0, stop=k == KC - 1)
                    else:
                        w = mwq if kind == "q" else mwk
                        if n == SPLIT[0]:
                            pe.wait_ge(m_task_free, i * MT + KC)
                        for k in range(KC):
                            last = nc.tensor.matmul(bank[:, :], w[:, k, c * P:(c + 1) * P], hnT[:, k, :],
                                                    start=k == 0, stop=k == KC - 1)
                    last.then_inc(m_task_done, 1)

                def score(i, u):
                    h, t = u // NT, u % NT
                    if u % 8 == 0:
                        pe.wait_ge(m_split, i * len(SPLIT) + 2 * (h // 2) + 2)
                        pe.wait_ge(m_k_doubled, i * MPAIRS + h // 2 + 1)
                    if not (isinstance(i, int) and i == 0 and u < 2):
                        pe.wait_ge(m_masked, i * UNITS + u - 1)
                    for part in range(2):
                        last = nc.tensor.matmul(s_ps[u % 2][:, :], q_parts[:, h, t * P:(t + 1) * P], k_parts[:, part, h, :],
                                                start=part == 0, stop=part == 1)
                    last.then_inc(m_score_done, 1)

                def turn_probs(i, u):
                    pe.wait_ge(m_prob_ready, i * UNITS + u + 1)
                    if not (isinstance(i, int) and i == 0 and u < 2):
                        pe.wait_ge(m_probT_ready, i * UNITS + u - 1)
                    for k in range(NT):
                        last = nc.tensor.transpose(pt_ps[u % 2][:, k * P:(k + 1) * P], probs[:, u % 3, k * P:(k + 1) * P], ident[:, :])
                    last.then_inc(m_turned, 1)

                def context(i, s, q):
                    pe.wait_ge(m_probT_ready, i * UNITS + 8 * q + 8)
                    if q == 0:
                        pe.wait_ge(m_task_free, i * MT + MTASKS.index(("v", NT - 1)) + 1)
                    pe.wait_ge(m_ctx_ready, i * MPAIRS + q + 1)
                    for k in range(NT):
                        for a in range(2):
                            h = 2 * q + a
                            last = nc.tensor.matmul(ctx_ps[64 * a:64 * a + 64, :], mv_tile[:, s, k, h * MD:(h + 1) * MD],
                                                    probT[:, (s + q) % 2, a, k, :], start=k == 0, stop=k == NT - 1,
                                                    tile_position=(0, 64 * a))
                    last.then_inc(m_pv_done, 1)

                def project(i, t):
                    if t == 0:
                        pe.wait_ge(m_ctx_ready, i * MPAIRS + MPAIRS + 1)
                    pe.wait_ge(m_out_read, i * NT + t + 1)
                    nc.tensor.matmul(out_ps[:, 0:D], onesb[:, :], brow[:, 0:D], start=True, stop=False)
                    for c in range(KC):
                        last = nc.tensor.matmul(out_ps[:, 0:D], ctxT[:, c, t * P:(t + 1) * P], mwf[:, c, :],
                                                start=False, stop=c == KC - 1)
                    last.then_inc(m_out_done, 1)

                def pre(i, s):
                    for n in range(MT):
                        mtask(i, s, n)
                    score(i, 0)

                def at(i, s, u, prev, nxt):
                    if u < UNITS - 1:
                        score(i, u + 1)
                    elif nxt:
                        score(i + 1, 0)
                    if nxt and u in TASK_AT:
                        mtask(i + 1, 1 - s, TASK_AT[u])
                    if prev and u in LATE_AT:
                        mtask(i, s, LATE_AT[u])
                    if prev and u in OUT_AT:
                        project(i - 1, OUT_AT[u])
                    if u >= TURN:
                        turn_probs(i, u - TURN)
                    elif prev:
                        turn_probs(i - 1, u - TURN + UNITS)
                    if u >= AT_PV and (u - AT_PV) % 8 == 0:
                        context(i, s, (u - AT_PV) // 8)
                    elif prev and (u + UNITS - AT_PV) // 8 == 2 and (u + UNITS - AT_PV) % 8 == 0:
                        context(i - 1, 1 - s, 2)

                def drain(i, s):
                    for u in range(UNITS - TURN, UNITS):
                        turn_probs(i, u)
                    context(i, s, 2)
                    for t in range(NT):
                        project(i, t)

                mha_units(pe, pre, at, drain)

            walk(pe, gat, mha)

        @block.scalar
        def _(act):
            act.sem_inc(acc_free, 1)
            act.sem_inc(m_ctx_ready, 1)
            act.wait_ge(const_done, 1)
            nc.scalar.activation(sel[:, :, :], selF, ACT.Copy).then_inc(sel_ready, 1)

            def normalize(i, s):
                act.wait_ge(nmr_ready, i + 1)
                act.wait_ge(hn_used, i) if not (isinstance(i, int) and i == 0) else None
                for t in range(NT):
                    last = nc.scalar.activation(hn[:, t, :], xin[:, s, t, :], ACT.Relu, bias=nmr[:, t:t + 1], scale=rstd[:, t:t + 1])
                last.then_inc(hn_ready, 1)

            def empty(i, s, k):
                bank = ring[k % 2]
                act.wait_ge(task_done, i * TASKS + k + 1)
                if k < T_H:
                    last = nc.scalar.activation(hnT[:, k, :], bank[:, :], ACT.Copy)
                elif k < T_HT[0]:
                    if k == T_H and not (isinstance(i, int) and i == 0):
                        act.wait_ge(vals_ready, i)
                    last = nc.scalar.activation(hb[:, k - T_H, :], bank[:, 0:D], ACT.Copy)
                elif k in T_Z:
                    if k == T_Z[0] and not (isinstance(i, int) and i == 0):
                        act.wait_ge(res_ready, i)
                    last = nc.scalar.activation(gate[:, s, T_Z.index(k), :], bank[:, 0:D], ACT.Tanh, scale=0.5)
                elif k in T_HT:
                    last = nc.scalar.activation(thT[:, T_HT.index(k), :], bank[:, :], ACT.Tanh, bias=nb1[:, :])
                elif k == T_SD:
                    act.wait_ge(dmax_ready, i + 1)
                    nc.scalar.activation(rows[Q1:Q1 + H, :], bank[Q1:Q1 + H, :], ACT.Exp, bias=dm[Q1:Q1 + H, 1:2], scale=0.8)
                    nc.scalar.activation(rows[Q2:Q2 + H, :], bank[Q1:Q1 + H, :], ACT.Exp, bias=dm[Q1:Q1 + H, 2:3], scale=0.2)
                    last = nc.scalar.activation(rr[0:H, :], bank[0:H, :], ACT.Relu, bias=dm[0:H, 0:1])
                else:
                    nc.scalar.activation(ucol[:, s, :, :], bank.rearrange("p (t c) -> p t c", t=NT)[:, :, Q1:Q1 + H], ACT.Copy)
                    nc.scalar.activation(dcol[:, :, :], bank.rearrange("p (t c) -> p t c", t=NT)[:, :, Q2:Q2 + H], ACT.Copy)
                    last = nc.scalar.activation(vals[:, s, :, :, E], bank.rearrange("p (t c) -> p t c", t=NT)[:, :, Q2:Q2 + H], ACT.Copy)
                last.then_inc(task_free, 1)
                if k == T_SD:
                    act.wait_ge(task_free, i * TASKS + T_SD + 1)
                    nc.scalar.activation(rows[0:H, :], rr[0:H, :], ACT.Exp, scale=-0.8).then_inc(rows_ready, 1)
                    act.wait_ge(rows_ready, i + 1)
                    nc.scalar.activation(vparts[0:H, s, :], rows[0:H, :], ACT.Copy).then_inc(vhi_ready, 1)

            def copy_acc(i, p):
                act.wait_ge(acc_done, i * PAIRS + p + 1)
                if not (isinstance(i, int) and i == 0 and p < 2):
                    act.wait_ge(back_done, i * PAIRS + p)
                nc.scalar.activation(accT[:, p % 2, :], acc[:, :], ACT.Copy).then_inc(acc_free, 1)

            def exps(i, s):
                act.wait_ge(o1_ready, i * PAIRS + PAIRS + 1)
                if not (isinstance(i, int) and i == 0):
                    act.wait_ge(res_ready, i + 1)
                nc.scalar.activation(ex[:, :, :], o1[:, s, :, :], ACT.Exp, bias=minus1[:, :]).then_inc(exp_done, 1)

            def gat(base, layer, src, off):
                def pre(i, s):
                    normalize(i, s)
                    for k in range(TASKS):
                        if k == T_HT[0]:
                            act.wait_ge(bias_done, layer + 1)
                        if k == T_SD:
                            normalize(i + 1, 1 - s)
                            act.wait_ge(vals_cleared, layer + 1)
                        empty(i, s, k)

                def slot(i, s, p, prev, nxt):
                    if p == 2 and prev:
                        exps(i - 1, 1 - s)
                    if p >= 1:
                        copy_acc(i, p - 1)
                    elif prev:
                        copy_acc(i - 1, PAIRS - 1)
                    if nxt:
                        for k in SLOT_TASKS[p]:
                            empty(i + 1, 1 - s, k)
                    if nxt == 2 and p == 5:
                        normalize(i + 2, s)

                def drain(i, s):
                    copy_acc(i, PAIRS - 1)
                    exps(i, s)

                gat_slots(act, base, pre, slot, drain)

            def mha(src, before):
                act.wait_ge(m_bias_done, 1)

                def normalize(i, s, tiles=range(NT)):
                    act.wait_ge(m_nmr_ready, i + 1)
                    for t in tiles:
                        last = nc.scalar.activation(hn[:, t, :], xin[:, s, t, :], ACT.Relu, bias=nmr[:, t:t + 1], scale=rstd[:, t:t + 1])
                    if tiles[-1] == NT - 1:
                        last.then_inc(m_hn_ready, 1)

                def empty(i, s, n):
                    kind, c = MTASKS[n]
                    bank = mring[n % 2]
                    act.wait_ge(m_task_done, i * MT + n + 1)
                    if kind == "hT":
                        last = nc.scalar.activation(hnT[:, c, :], bank[:, :], ACT.Copy)
                    elif kind == "v":
                        last = nc.scalar.activation(mv_tile[:, s, c, :], bank[:, 0:D], ACT.Copy)
                    else:
                        for a in range(2):
                            own = slice(64 * a, 64 * a + 64)
                            if kind == "q":
                                last = nc.scalar.activation(q_parts[own, 2 * c + a, :], bank[own, :], ACT.Identity,
                                                            bias=mbias[own, 0, c:c + 1])
                            else:
                                for to in (slice(0, 64), slice(64, P)):
                                    last = nc.scalar.activation(k_parts[to, 0, 2 * c + a, :], bank[own, :], ACT.Identity,
                                                                bias=mbias[own, 1, c:c + 1])
                    last.then_inc(m_task_free, 1)

                def double_low(i, n):
                    c = MTASKS[n][1]
                    act.wait_ge(m_split, i * len(SPLIT) + SPLIT.index(n) + 1)
                    for a in range(2):
                        own, other = slice(64 * a, 64 * a + 64), slice(64 * (1 - a), 64 * (1 - a) + 64)
                        last = nc.scalar.activation(k_parts[other, 1, 2 * c + a, :],
                                                    k_parts[own, 1, 2 * c + a, :].bitcast(F32), ACT.Copy)
                    last.then_inc(m_k_doubled, 1)

                def exp(i, u):
                    act.wait_ge(m_masked, i * UNITS + u + 1)
                    if not (isinstance(i, int) and i == 0 and u < 3):
                        act.wait_ge(m_prob_ready, i * UNITS + u - 2)
                    r = u % 3
                    nc.scalar.activation(expd[:, r, :], scores[:, r, :], ACT.Exp, bias=nmax[:, r:r + 1], scale=-1.0,
                                         accum_out=rsum[:, r:r + 1]).then_inc(m_exp_done, 1)

                def copy_ctx(i, q):
                    act.wait_ge(m_pv_done, i * MPAIRS + q + 2)
                    if q == 0:
                        act.wait_ge(m_out_done, i * NT + 1)
                    nc.scalar.activation(ctxT[:, q, :], ctx_ps[:, :], ACT.Identity, bias=mbias[:, 2, q:q + 1]).then_inc(m_ctx_ready, 1)

                def pre(i, s):
                    normalize(i, s)
                    for n in range(MT):
                        empty(i, s, n)
                        if MTASKS[n][0] == "k":
                            double_low(i, n)

                def at(i, s, u, prev, nxt):
                    exp(i, u)
                    for due, n in tuple(TASK_AT.items()) + tuple(LATE_AT.items()):
                        if MTASKS[n][0] != "k" or (due + 3) % UNITS != u:
                            continue
                        if n in TASK_AT.values() and due + 3 < UNITS:
                            if nxt:
                                double_low(i + 1, n)
                        elif prev:
                            double_low(i, n)
                    if nxt and u == AT_STATS + 2:
                        normalize(i + 1, 1 - s, range(2))
                    if nxt and u == AT_STATS + 3:
                        normalize(i + 1, 1 - s, range(2, NT))
                    if nxt and u in TASK_AT:
                        empty(i + 1, 1 - s, TASK_AT[u])
                    if prev and u in LATE_AT:
                        empty(i, s, LATE_AT[u])
                    if u >= AT_PV and (u - AT_PV) % 8 == 0:
                        copy_ctx(i, (u - AT_PV) // 8)
                    elif prev and u == AT_PV + 16 - UNITS:
                        copy_ctx(i - 1, 2)

                mha_units(act, pre, at, lambda i, s: copy_ctx(i, 2))

            walk(act, gat, mha)

        @block.vector
        def _(dve):
            dve.sem_inc(o1_ready, 1)
            dve.sem_inc(res_ready, 1)
            dve.sem_inc(m_out_read, 1)
            nc.vector.memset(rows[:, :], 0.0)
            nc.vector.memset(vparts[:, :, :].bitcast(F32), 0.0)
            nc.vector.memset(brow[:, :], 0.0)
            nc.vector.memset(onesb[:, :], 0.0)
            nc.vector.memset(minus1[:, :], -1.0).then_inc(const_step, 1)
            dve.wait_ge(const_step, 1)
            for q in (Q0, Q1):
                nc.vector.memset(onesb[q:q + 1, :], 1.0)
            nc.vector.memset(onesb[Q2:Q2 + 1, :], 1.0).then_inc(const_step, 1)

            def ln_stats(s, loads, n, stats_done, aggr_done, var_done):
                dve.wait_ge(x_in[s], loads)
                for t in range(NT):
                    last = nc.vector.bn_stats(st6[:, t, :], xin[:, s, t, :])
                last.then_inc(stats_done, 1)
                dve.wait_ge(stats_done, n)
                met(dve)
                for t in range(NT):
                    last = nc.vector.bn_aggr(mv[:, t, :], st6[:, t, :])
                last.then_inc(aggr_done, 1)
                dve.wait_ge(aggr_done, n)
                nc.vector.tensor_scalar(veps[:, :], mv[:, :, 1], EPS, None, ALU.add).then_inc(var_done, 1)

            def bias_rows(layer):
                n = [layer * 6]

                def link(ins):
                    n[0] = n[0] + 1
                    ins.then_inc(bias_step, 1)
                    dve.wait_ge(bias_step, n[0])

                dve.wait_ge(w_in, 64 * (layer + 1))
                nc.vector.tensor_scalar(nb1[:, :], nb1[:, :], -1.0, -1.0, ALU.mult, ALU.add)
                link(nc.vector.tensor_scalar(biasf[:, 0, 0:D], biasf[:, 0, 0:D], 1.0, None, ALU.add))
                link(nc.vector.tensor_copy(brow[0:1, :], biasf[:, 0, :]))
                link(nc.vector.tensor_tensor(biasf[:, 1, :], biasf[:, 0, :], brow[0:1, :], ALU.subtract))
                link(nc.vector.tensor_copy(biasp[:, 0, :], biasf[:, 1, :]))
                link(nc.vector.tensor_tensor(biasf[:, 2, :], biasf[:, 1, :], biasp[:, 0, :], ALU.subtract))
                link(nc.vector.tensor_copy(brow[Q1:Q1 + 1, :], biasp[:, 0, :]))
                nc.vector.tensor_copy(brow[Q2:Q2 + 1, :], biasf[:, 2, :]).then_inc(bias_done, 1)

            def neg_mean(i):
                dve.wait_ge(rstd_ready, i + 1)
                nc.vector.scalar_tensor_tensor(out=nmr[:, :], in0=mv[:, :, 0], scalar=-1.0, in1=rstd[:, :],
                                               op0=ALU.mult, op1=ALU.mult).then_inc(nmr_ready, 1)

            def dmax(i):
                sd = ring[T_SD % 2]
                dve.wait_ge(task_done, i * TASKS + T_SD + 1)
                nc.vector.tensor_reduce(dm[Q1:Q1 + H, 0:1], sd[Q1:Q1 + H, :], AX_X, ALU.max).then_inc(dmax_done, 1)
                dve.wait_ge(dmax_done, i + 1)
                nc.vector.tensor_scalar(dm[Q1:Q1 + H, 1:2], dm[Q1:Q1 + H, 0:1], -0.8, None, ALU.mult)
                nc.vector.tensor_scalar(dm[Q1:Q1 + H, 2:3], dm[Q1:Q1 + H, 0:1], -0.2, None, ALU.mult)
                nc.vector.tensor_copy(dm[0:H, 0:1], dm[Q1:Q1 + H, 0:1]).then_inc(dmax_ready, 1)

            def v_low(i, s):
                dve.wait_ge(vhi_ready, i + 1)
                nc.vector.tensor_tensor(vparts[Q1:Q1 + H, s, :], rows[0:H, :], vparts[0:H, s, :].bitcast(F32),
                                        ALU.subtract).then_inc(vlo_ready, 1)

            def values(i, s):
                dve.wait_ge(task_free, i * TASKS + T_COL + 1)
                nc.vector.tensor_tensor(vals[:, s, :, :, 0:E], hb[:, :, :].rearrange("p t (a e) -> p t a e", e=E),
                                        dcol[:, :, :].unsqueeze(3).to_broadcast([P, NT, H, E]),
                                        ALU.mult).then_inc(vals_ready, 1)

            def weights(i, s, a):
                dve.wait_ge(vbc_done, i * H + a + 1)
                if a % 2 == 0 and not (isinstance(i, int) and i == 0 and a < 4):
                    dve.wait_ge(acc_done, i * PAIRS + a // 2 - 1)
                for t in range(NT):
                    last = nc.vector.scalar_tensor_tensor(out=wts[:, a // 2 % 2, a % 2, t, :], in0=vbc[a % 4][:, :],
                                                          scalar=ucol[:, s, t, a:a + 1], in1=maskb[:, s, t, :],
                                                          op0=ALU.max, op1=ALU.mult)
                last.then_inc(wts_ready, 1)

            def divide(i, s, p):
                g = i * PAIRS + p + 1
                b4 = back.rearrange("p (t a c) -> p t a c", t=NT, a=2)
                dve.wait_ge(back_done, g + 1)
                nc.vector.reciprocal(rcp[:, :, :], b4[:, :, :, E]).then_inc(rcp_done, 1)
                dve.wait_ge(rcp_done, g)
                nc.vector.tensor_tensor(o1[:, s, :, 2 * p * E:(2 * p + 2) * E].rearrange("p t (a e) -> p t a e", e=E),
                                        b4[:, :, :, 0:E], rcp[:, :, :].unsqueeze(3).to_broadcast([P, NT, 2, E]),
                                        ALU.mult).then_inc(o1_ready, 1)

            def finish(i, s, off):
                dve.wait_ge(exp_done, i + 1)
                nc.vector.scalar_tensor_tensor(out=ex[:, :, :], in0=ex[:, :, :], scalar=1.0, in1=o1[:, s, :, :],
                                               op0=ALU.min, op1=ALU.max).then_inc(elu_done, 1)
                dve.wait_ge(elu_done, i + 1)
                dve.wait_ge(skip_ready, i + 1)
                nc.vector.tensor_tensor(ex[:, :, :], ex[:, :, :], gate[:, s, :, :], ALU.mult).then_inc(gated, 1)
                dve.wait_ge(gated, i + 1)
                dve.wait_ge(stored, (i + off) * 16 + 1)
                nc.vector.tensor_tensor(res[:, :, :], ex[:, :, :], skip[:, s, :, :], ALU.add).then_inc(res_ready, 1)

            def gat(base, layer, src, off):

                def nth(i, s):
                    return 8 * (i + off - s) + 16

                def pre(i, s):
                    stats(i, s)
                    neg_mean(i)
                    bias_rows(layer)
                    stats(i + 1, 1 - s)
                    neg_mean(i + 1)
                    dve.wait_ge(mask_in[s], nth(i, s))
                    dmax(i)
                    v_low(i, s)
                    values(i, s)

                def stats(i, s):
                    ln_stats(s, nth(i, s), i + 1, bn_stats_done, bn_aggr_done, var_ready)

                def slot(i, s, p, prev, nxt):
                    if p == 0 and prev:
                        dve.wait_ge(mask_in[s], nth(i, s))
                    weights(i, s, 2 * p)
                    if p >= 2:
                        divide(i, s, p - 2)
                    elif prev:
                        divide(i - 1, 1 - s, PAIRS + p - 2)
                    if p == 4 and nxt == 2:
                        stats(i + 2, s)
                    if p == 5 and nxt == 2:
                        neg_mean(i + 2)
                    if p == 5 and nxt:
                        v_low(i + 1, 1 - s)
                    weights(i, s, 2 * p + 1)
                    if p == 4 and nxt:
                        dmax(i + 1)
                    if p == 2 and prev:
                        finish(i - 1, 1 - s, off)
                    if p == 5 and nxt:
                        values(i + 1, 1 - s)

                def drain(i, s):
                    divide(i, s, PAIRS - 2)
                    divide(i, s, PAIRS - 1)
                    finish(i, s, off)

                gat_slots(dve, base, pre, slot, drain)

            def mha(src, before):
                dve.wait_ge(m_w_in, 16 * 6)
                made = [0]

                def link(ins):
                    made[0] += 1
                    ins.then_inc(m_bias_step, 1)
                    dve.wait_ge(m_bias_step, made[0])

                nc.vector.tensor_scalar(mwq, mwq, 0.125, None, ALU.mult)
                nc.vector.tensor_scalar(mbias[:, 0, :], mbias[:, 0, :], 0.125, None, ALU.mult)
                link(nc.vector.tensor_copy(brow[0:1, 0:D], biasf[:, 0, 0:D]))
                link(nc.vector.tensor_tensor(biasf[:, 1, 0:D], biasf[:, 0, 0:D], brow[0:1, 0:D], ALU.subtract))
                link(nc.vector.tensor_copy(biasp[:, 0, 0:D], biasf[:, 1, 0:D]))
                link(nc.vector.tensor_tensor(biasf[:, 2, 0:D], biasf[:, 1, 0:D], biasp[:, 0, 0:D], ALU.subtract))
                link(nc.vector.tensor_copy(brow[Q1:Q1 + 1, 0:D], biasp[:, 0, 0:D]))
                nc.vector.tensor_copy(brow[Q2:Q2 + 1, 0:D], biasf[:, 2, 0:D]).then_inc(m_bias_done, 1)

                def stats(i, s):
                    ln_stats(s, 8 * (i + before - s) + 16, i + 1, m_stats_done, m_aggr_done, m_var_ready)

                def neg_mean(i):
                    dve.wait_ge(m_rstd_ready, i + 1)
                    nc.vector.scalar_tensor_tensor(out=nmr[:, :], in0=mv[:, :, 0], scalar=-1.0, in1=rstd[:, :],
                                                   op0=ALU.mult, op1=ALU.mult).then_inc(m_nmr_ready, 1)

                def split(i, n):
                    kind, c = MTASKS[n]
                    bank = mring[n % 2]
                    dve.wait_ge(m_task_free, i * MT + n + 1)
                    for a in range(2):
                        own, other = slice(64 * a, 64 * a + 64), slice(64 * (1 - a), 64 * (1 - a) + 64)
                        if kind == "q":
                            last = nc.vector.scalar_tensor_tensor(out=q_parts[other, 2 * c + a, :], in0=bank[own, :],
                                                                  scalar=mbias[own, 0, c:c + 1],
                                                                  in1=q_parts[own, 2 * c + a, :].bitcast(F32),
                                                                  op0=ALU.add, op1=ALU.subtract)
                        else:
                            last = nc.vector.scalar_tensor_tensor(out=k_parts[own, 1, 2 * c + a, :], in0=bank[own, :],
                                                                  scalar=mbias[own, 1, c:c + 1],
                                                                  in1=k_parts[own, 0, 2 * c + a, :].bitcast(F32),
                                                                  op0=ALU.add, op1=ALU.subtract)
                    last.then_inc(m_split, 1)

                def masked(i, s, u):
                    if u == 0:
                        dve.wait_ge(m_negm_ready, i + 1)
                    dve.wait_ge(m_score_done, i * UNITS + u + 1)
                    if not (isinstance(i, int) and i == 0 and u < 3):
                        dve.wait_ge(m_exp_done, i * UNITS + u - 2)
                    met(dve)
                    r = u % 3
                    nc.vector.tensor_tensor_reduce(out=scores[:, r, :], in0=s_ps[u % 2][:, :], in1=negm[:, s, u % NT, :],
                                                   scale=-1.0, scalar=3e38, op0=ALU.add, op1=ALU.min,
                                                   accum_out=nmax[:, r:r + 1]).then_inc(m_masked, 1)

                def invert(i, u):
                    dve.wait_ge(m_exp_done, i * UNITS + u + 1)
                    if not (isinstance(i, int) and i == 0 and u < 3):
                        dve.wait_ge(m_prob_ready, i * UNITS + u - 2)
                    nc.vector.reciprocal(rinv[:, u % 3:u % 3 + 1], rsum[:, u % 3:u % 3 + 1]).then_inc(m_rinv_ready, 1)

                def copy_probT(i, s, u):
                    h, t = u // NT, u % NT
                    q = h // 2
                    dve.wait_ge(m_turned, i * UNITS + u + 1)
                    if u % 8 == 0 and not (isinstance(i, int) and i == 0 and q < 2):
                        dve.wait_ge(m_pv_done, i * MPAIRS + q)
                    nc.vector.tensor_copy(probT[:, (s + q) % 2, h % 2, :, t * P:(t + 1) * P],
                                          pt_ps[u % 2].rearrange("p (k n) -> p k n", k=NT)).then_inc(m_probT_ready, 1)

                def residual(i, t):
                    dve.wait_ge(m_out_done, i * NT + t + 2)
                    if t == 0:
                        dve.wait_ge(m_x_in, i * 16 + 16)
                    nc.vector.tensor_tensor(res[:, t, :], out_ps[:, 0:D], res[:, t, :], ALU.add).then_inc(m_out_read, 1)

                def pre(i, s):
                    dve.wait_ge(mask_in[s], 8 * (i + before - s) + 16)
                    stats(i, s)
                    neg_mean(i)
                    for n in SPLIT:
                        split(i, n)

                def at(i, s, u, prev, nxt):
                    masked(i, s, u)
                    if u >= 1:
                        invert(i, u - 1)
                    elif prev:
                        invert(i - 1, UNITS - 1)
                    if u > TURN:
                        copy_probT(i, s, u - TURN - 1)
                    elif prev:
                        copy_probT(i - 1, 1 - s, u - TURN - 1 + UNITS)
                    if prev and u in OUT_AT:
                        residual(i - 1, OUT_AT[u])
                    if nxt and TASK_AT.get(u - 2) in SPLIT:
                        split(i + 1, TASK_AT[u - 2])
                    if prev and TASK_AT.get(u - 2 + UNITS) in SPLIT:
                        split(i, TASK_AT[u - 2 + UNITS])
                    if prev and LATE_AT.get(u - 2) in SPLIT:
                        split(i, LATE_AT[u - 2])
                    if nxt and u == AT_STATS:
                        stats(i + 1, 1 - s)
                    if nxt and u == AT_STATS + 1:
                        neg_mean(i + 1)

                def drain(i, s):
                    invert(i, UNITS - 1)
                    for u in range(UNITS - TURN - 1, UNITS):
                        copy_probT(i, s, u)
                    for t in range(NT):
                        residual(i, t)

                mha_units(dve, pre, at, drain)

            walk(dve, gat, mha)

        @block.gpsimd
        def _(pool):
            made = [0]

            def link(ins):
                made[0] += 1
                ins.then_inc(pool_const, 1)
                pool.wait_ge(pool_const, made[0])

            link(nc.gpsimd.memset(ident[:, :], 0.0))
            link(nc.gpsimd.memset(selF, 0.0))
            link(nc.gpsimd.memset(wsd[:, :, :], 0.0))
            link(nc.gpsimd.memset(mhalf[:, :], -0.5))
            link(nc.gpsimd.affine_select(out=ident[:, :], in_=ident[:, :], compare_op=ALU.not_equal, fill=1.0,
                                         base=0, pattern=[[-1, P]], channel_multiplier=1))
            for q in (Q0, Q1):
                link(nc.gpsimd.affine_select(out=selF, in_=selF, compare_op=ALU.not_equal, fill=1.0, base=-q,
                                             pattern=[[-1, H], [0, P]], channel_multiplier=1))
            pool.wait_ge(const_step, 2)
            pool.sem_inc(const_done, 1)

            def rsqrt(i):
                pool.wait_ge(var_ready, i + 1)
                nc.gpsimd.tensor_tensor(rstd[:, :], veps[:, :], mhalf[:, :], ALU.pow).then_inc(rstd_ready, 1)

            def skip_early(i, s):
                pool.wait_ge(hn_ready, i + 1)
                if not (isinstance(i, int) and i == 0):
                    pool.wait_ge(res_ready, i)
                nc.gpsimd.tensor_tensor(skip[:, s, :, :], xin[:, s, :, :], hn[:, :, :], ALU.add).then_inc(xh_done, 1)
                if not (isinstance(i, int) and i == 0):
                    pool.wait_ge(skip_ready, i)
                    met(pool)
                nc.gpsimd.tensor_scalar(hn1[:, :, :], hn[:, :, :], 1.0, 1.0, ALU.add, ALU.mult).then_inc(hn_used, 1)

            def skip_late(i, s):
                pool.wait_ge(task_free, i * TASKS + T_Z[-1] + 1)
                pool.wait_ge(hn_used, i + 1)
                met(pool)
                nc.gpsimd.tensor_scalar(gate[:, s, :, :], gate[:, s, :, :], 0.5, 0.5, ALU.mult, ALU.add).then_inc(gate_half, 1)
                pool.wait_ge(gate_half, i + 1)
                nc.gpsimd.tensor_tensor(hn1[:, :, :], hn1[:, :, :], gate[:, s, :, :], ALU.mult).then_inc(gate_prod, 1)
                pool.wait_ge(gate_prod, i + 1)
                pool.wait_ge(xh_done, i + 1)
                nc.gpsimd.tensor_tensor(skip[:, s, :, :], skip[:, s, :, :], hn1[:, :, :], ALU.subtract).then_inc(skip_ready, 1)

            def gat(base, layer, src, off):
                def pre(i, s):
                    rsqrt(i)
                    pool.wait_ge(rstd_ready, i + 1)
                    pool.wait_ge(w_in, 64 * (layer + 1))
                    met(pool)
                    for c in range(KC):
                        for j in range(4):
                            a = 4 * c + j
                            last = nc.gpsimd.tensor_copy(wsd[32 * j:32 * j + 32, c, a:a + 33:32], wcol[32 * j:32 * j + 32, c, :])
                    last.then_inc(wprep_pool, 1)
                    pool.wait_ge(wprep_pool, layer + 1)
                    pool.wait_ge(hn_ready, i + 1)
                    rsqrt(i + 1)
                    skip_early(i, s)
                    nc.gpsimd.memset(vals[:, :, :, :, :], 0.0).then_inc(vals_cleared, 1)

                def slot(i, s, p, prev, nxt):
                    if p == 4 and nxt == 2:
                        rsqrt(i + 2)
                    if p == 0:
                        skip_late(i, s)
                    if p == 1 and nxt:
                        skip_early(i + 1, 1 - s)

                gat_slots(pool, base, pre, slot, lambda i, s: None)

            def mha(src, before):
                pool.wait_ge(m_w_in, 16 * 6)

                def rsqrt(i):
                    pool.wait_ge(m_var_ready, i + 1)
                    nc.gpsimd.tensor_tensor(rstd[:, :], veps[:, :], mhalf[:, :], ALU.pow).then_inc(m_rstd_ready, 1)

                def mask(i, s):
                    pool.wait_ge(mask_in[s], 8 * (i + before - s) + 16)
                    met(pool)
                    nc.gpsimd.tensor_scalar(negm[:, s, :, :], maskb[:, s, :, :], -1.0, -NEG, ALU.add, ALU.mult).then_inc(m_negm_ready, 1)

                def scale(i, u):
                    r = u % 3
                    pool.wait_ge(m_rinv_ready, i * UNITS + u + 1)
                    if not (isinstance(i, int) and i == 0 and u < 3):
                        pool.wait_ge(m_turned, i * UNITS + u - 2)
                    met(pool)
                    nc.gpsimd.tensor_scalar(probs[:, r, :], expd[:, r, :], rinv[:, r:r + 1], 1.0, ALU.mult, ALU.mult).then_inc(m_prob_ready, 1)

                def pre(i, s):
                    mask(i, s)
                    rsqrt(i)

                def at(i, s, u, prev, nxt):
                    if u >= 1:
                        scale(i, u - 1)
                    elif prev:
                        scale(i - 1, UNITS - 1)
                    if nxt and u == AT_STATS:
                        rsqrt(i + 1)
                    if nxt and u == AT_PV + 1:
                        mask(i + 1, 1 - s)

                mha_units(pool, pre, at, lambda i, s: scale(i, UNITS - 1))

            walk(pool, gat, mha)


def layout(inputs):
    import numpy as np

    def a(name):
        return np.asarray(inputs[name])

    gat = ("L0_gnn_", "L2_gnn_", "L3_gnn_")
    adj = a("adj")
    return {
        "x": np.ascontiguousarray(a("x")),
        "adj": np.ascontiguousarray(adj),
        "adj_t": np.ascontiguousarray(adj.transpose(0, 2, 1)),
        "gat_w": np.stack([np.concatenate([a(g + "W").transpose(1, 0, 2).reshape(D, D), a(g + "H_w").T], 1) for g in gat]),
        "gat_bias": np.stack([np.concatenate([np.tile(a(g + "b"), H), a(g + "H_b")])[None] for g in gat]),
        "gat_ws": np.stack([np.stack([a(g + "w_src").reshape(D), a(g + "w_dst").reshape(D)], 1) for g in gat]),
        "wq": a("L1_gnn_Wq"), "wk": a("L1_gnn_Wk"), "wv": a("L1_gnn_Wv"), "wf": a("L1_gnn_Wf"),
        "mha_bias": np.ascontiguousarray(np.stack([a("L1_gnn_" + n) for n in ("bq", "bk", "bv")]).reshape(3, KC, P).transpose(2, 0, 1)),
        "mha_bf": a("L1_gnn_bf")[None],
    }


def kernel(**inputs):
    import numpy as np
    import concourse.bacc as bacc
    from concourse import mybir as mb
    from concourse.bass_utils import run_bass_kernel_spmd

    arrays = layout(inputs)
    nc = bacc.Bacc("TRN2", target_bir_lowering=False, num_devices=1)
    aps = [nc.dram_tensor(n, v.shape, mb.dt.from_np(v.dtype), kind="ExternalInput").ap() for n, v in arrays.items()]
    out = nc.dram_tensor("out", (B, N, D), mb.dt.float32, kind="ExternalOutput").ap()
    program(nc, *aps, out)
    r = run_bass_kernel_spmd(nc, [arrays], core_ids=[0])
    return np.asarray(r.results[0]["out"])
```

```python
from contextlib import ExitStack

import concourse.bass as bass
from concourse import mybir

F32 = mybir.dt.float32
F32R = mybir.dt.float32r
BF16 = mybir.dt.bfloat16
U8 = mybir.dt.uint8
ALU = mybir.AluOpType
ACT = mybir.ActivationFunctionType
AX_X = mybir.AxisListType.X

P = 128
B = 16
N = 512
D = 384
NT = N // P
KC = D // P
H = 12
E = D // H
PAIRS = H // 2
MH = 6
MD = D // MH
EPS = 1e-5
NEG = -9000000000000000.0
Q0, Q1, Q2, Q3 = 0, 32, 64, 96

TASKS = 17
T_H = 3
T_HT = (7, 8, 10)
T_Z = (9, 13, 15, 16)
T_D, T_S, T_COL = 11, 12, 14
SLOT_TASKS = ((0, 1, 2), (3,), (4, 5, 6), (7, 8, 9, 10), (11, 12), (13, 14, 15, 16))
HC = P // E
ROWS = Q3

UNITS = MH * NT
MPAIRS = MH // 2
MTASKS = (("hT", 0), ("hT", 1), ("hT", 2), ("q", 0), ("k", 0), ("v", 0), ("v", 1), ("q", 1),
          ("k", 1), ("v", 2), ("v", 3), ("q", 2), ("k", 2))
MT = len(MTASKS)
SPLIT = tuple(n for n, (kind, c) in enumerate(MTASKS) if kind in "qk")
TASK_AT = {10: 0, 11: 1, 12: 2, 13: 3, 14: 4, 16: 5, 17: 6, 18: 7, 19: 8, 23: 9}
LATE_AT = {0: 10, 1: 11, 3: 12}
M_FIRST = 6
AT_STATS = 3
TURN = 3
AT_PV = 9 + TURN
OUT_AT = {6: 0, 7: 1, 8: 2, 9: 3}
CUT = 11


def program(nc, x, adj, adj_t, gat_w, gat_bias, gat_ws, wq, wk, wv, wf, mha_bias, mha_bf, out, passes=("g0", "m", "g2")):
    ctx = ExitStack()
    with ctx:
        def sb(name, shape, dt=F32):
            return ctx.enter_context(nc.sbuf_tensor(name, shape, dt))

        def sem(name):
            return ctx.enter_context(nc.semaphore(name))

        xin = sb("xin", [P, 2, NT, D])
        hn = sb("hn", [P, NT, D])
        hnT = sb("hnT", [P, KC, N])
        hn1 = sb("hn1", [P, NT, D])
        skip = sb("skip", [P, 2, NT, D])
        with nc.sbuf_tensor("gate", [P, 2, NT, D], F32) as gate:
            pass
        q_parts = sb("q_parts", [P, MH, N], F32R)
        with nc.sbuf_tensor("vals", [P, 2, NT, H, 64], F32) as vals:
            pass
        k_parts = sb("k_parts", [P, 2, MH, N], F32R)
        hb = sb("hb", [P, NT, D])
        thT = sb("thT", [P, KC, N])
        ucol = sb("ucol", [P, 2, NT, H])
        dcol = sb("dcol", [P, NT, H])
        wts = sb("wts", [P, 2, 2, NT, N])
        accT = sb("accT", [P, 2, N])
        rcp = sb("rcp", [P, NT, 2])
        o1 = sb("o1", [P, 2, NT, D])
        ex = sb("ex", [P, NT, D])
        res = sb("res", [P, NT, D])
        rows = sb("rows", [P, N])
        vrow = sb("vrow", [P, N])
        vparts = sb("vparts", [P, 2, N], F32R)
        maskb = sb("maskb", [P, 2, NT, N], U8)
        wcat = sb("wcat", [P, KC, 2 * D])
        wcol = sb("wcol", [P, KC, 2])
        wsd = sb("wsd", [P, KC, 2, 32])
        wts_row = wts[0:1, :, :, :, :].rearrange("p r a t n -> p (r a t n)")
        biasf = wts_row[:, 0:6 * D].rearrange("p (k d) -> p k d", k=3)
        biasp = wts_row[:, 6 * D:7 * D].bitcast(BF16).rearrange("p (k d) -> p k d", k=1)
        brow = sb("brow", [P, 2 * D], BF16)
        nb1 = sb("nb1", [P, 1])
        onesb = sb("onesb", [P, P], BF16)
        ident = sb("ident", [P, P])
        sel = sb("sel", [P, H, P], F32R)
        st6 = sb("st6", [P, NT, 6])
        mv = sb("mv", [P, NT, 2])
        veps = sb("veps", [P, NT])
        mhalf = sb("mhalf", [P, NT])
        minus1 = sb("minus1", [P, 1])
        rstd = sb("rstd", [P, NT])
        nmr = sb("nmr", [P, NT])
        dm = sb("dm", [P, 2])
        slope = sb("slope", [P, 1])
        low = sb("low", [P, 1])
        mwf = sb("mwf", [P, KC, D])
        negm = sb("negm", [P, 2, NT, N])
        mbias = sb("mbias", [P, 3, KC])
        nmax = sb("nmax", [P, 3])
        rsum = sb("rsum", [P, 3])
        rinv = sb("rinv", [P, 3])
        mwq, mwk = wcat[:, :, 0:D], wcat[:, :, D:2 * D]
        mwv = hb[:, 0:KC, :]
        mv_tile = skip
        probT = wts
        ctxT = thT
        scores = o1[:, 0, :, :].rearrange("p t d -> p (t d)").rearrange("p (r n) -> p r n", r=3)
        expd = ex[:, :, :].rearrange("p t d -> p (t d)").rearrange("p (r n) -> p r n", r=3)
        probs = hn1[:, :, :].rearrange("p t d -> p (t d)").rearrange("p (r n) -> p r n", r=3)
        selF = ex[:, :, :].rearrange("p t (a c) -> p (t a) c", c=P)
        banks = [ctx.enter_context(nc.psum_tensor(f"bank{i}", [P, 512], F32))[:, :] for i in range(8)]
        vbc, acc, back, ring = banks[0:4], banks[4], banks[5], banks[6:8]
        s_ps, pt_ps, ctx_ps, mring, out_ps = banks[0:2], banks[2:4], banks[4], banks[5:7], banks[7]

        x_in = [sem("x_in0"), sem("x_in1")]
        mask_in = [sem("mask_in0"), sem("mask_in1")]
        stored = sem("stored")
        w_in = sem("w_in")
        const_step = sem("const_step")
        waits_met = {e.engine: sem(n + "_waits_met") for n, e in (("dve", nc.vector), ("pool", nc.gpsimd), ("sp", nc.sync), ("act", nc.scalar))}
        const_done = sem("const_done")
        sel_ready = sem("sel_ready")
        wprep_pool = sem("wprep_pool")
        pool_const = sem("pool_const")
        bias_step = sem("bias_step")
        bias_done = sem("bias_done")
        bn_stats_done = sem("bn_stats_done")
        bn_aggr_done = sem("bn_aggr_done")
        var_ready = sem("var_ready")
        rstd_ready = sem("rstd_ready")
        nmr_ready = sem("nmr_ready")
        hn_ready = sem("hn_ready")
        xh_done = sem("xh_done")
        hn_used = sem("hn_used")
        gate_half = sem("gate_half")
        gate_prod = sem("gate_prod")
        skip_ready = sem("skip_ready")
        task_done = sem("task_done")
        task_free = sem("task_free")
        dmax_done = sem("dmax_done")
        dmax_ready = sem("dmax_ready")
        rows_ready = sem("rows_ready")
        vhi_ready = sem("vhi_ready")
        vlo_ready = sem("vlo_ready")
        vals_cleared = sem("vals_cleared")
        vals_ready = sem("vals_ready")
        vbc_done = sem("vbc_done")
        wts_ready = sem("wts_ready")
        acc_done = sem("acc_done")
        acc_free = sem("acc_free")
        back_done = sem("back_done")
        rcp_done = sem("rcp_done")
        o1_ready = sem("o1_ready")
        exp_done = sem("exp_done")
        elu_done = sem("elu_done")
        gated = sem("gated")
        res_ready = sem("res_ready")

        m_w_in = sem("m_w_in")
        m_bf_in = sem("m_bf_in")
        m_scaled = sem("m_scaled")
        m_bias_done = sem("m_bias_done")
        m_bias_step = sem("m_bias_step")
        m_stats_done = sem("m_stats_done")
        m_aggr_done = sem("m_aggr_done")
        m_var_ready = sem("m_var_ready")
        m_rstd_ready = sem("m_rstd_ready")
        m_nmr_ready = sem("m_nmr_ready")
        m_hn_ready = sem("m_hn_ready")
        m_task_done = sem("m_task_done")
        m_task_free = sem("m_task_free")
        m_split = sem("m_split")
        m_k_doubled = sem("m_k_doubled")
        m_negm_ready = sem("m_negm_ready")
        m_x_in = sem("m_x_in")
        m_score_done = sem("m_score_done")
        m_masked = sem("m_masked")
        m_exp_done = sem("m_exp_done")
        m_rinv_ready = sem("m_rinv_ready")
        m_prob_ready = sem("m_prob_ready")
        m_turned = sem("m_turned")
        m_probT_ready = sem("m_probT_ready")
        m_pv_done = sem("m_pv_done")
        m_ctx_ready = sem("m_ctx_ready")
        m_out_done = sem("m_out_done")
        m_out_read = sem("m_out_read")

        block = ctx.enter_context(nc.Block())

        def nodes(ap):
            return ap.rearrange("(t p) d -> p t d", p=P)

        def met(eng):
            eng.sem_inc(waits_met[eng.engine], 1)

        def first_graphs_stored(eng, graphs, n):
            if not isinstance(graphs, int) or graphs > 0:
                eng.wait_ge(stored, (graphs - B + n) * 16 + 1)

        def walk(eng, gat, mha):
            n = 0
            if "g0" in passes:
                gat(0, 0, x, 0)
                n += B
            if "m" in passes:
                mha(out if n else x, n)
                n += B
            if "g2" in passes:
                with eng.Fori(0, 2) as l:
                    gat(l * B + B, l + 1, out, n - B)

        def mha_units(eng, pre, at, drain):
            pre(0, 0)
            for u in range(CUT):
                at(0, 0, u, False, True)
            with eng.Fori(0, B // 2 - 1) as j:
                for s in range(2):
                    i = j * 2 + s
                    for u in range(CUT, UNITS):
                        at(i, s, u, True, True)
                    for u in range(CUT):
                        at(i + 1, 1 - s, u, True, True)
            for u in range(CUT, UNITS):
                at(B - 2, 0, u, True, True)
            for u in range(UNITS):
                at(B - 1, 1, u, True, False)
            drain(B - 1, 1)

        def gat_slots(eng, base, pre, slot, drain):
            pre(base, 0)
            for p in range(3):
                slot(base, 0, p, False, 2)
            with eng.Fori(0, B // 2 - 1) as j:
                for s in range(2):
                    i = base + j * 2 + s
                    for p in range(3, PAIRS):
                        slot(i, s, p, True, 2)
                    for p in range(3):
                        slot(i + 1, 1 - s, p, True, 2)
            for p in range(3, PAIRS):
                slot(base + B - 2, 0, p, True, 1)
            for p in range(PAIRS):
                slot(base + B - 1, 1, p, True, 0)
            drain(base + B - 1, 1)

        @block.sync
        def _(sp):
            sp.sem_inc(stored, 1)

            def load_mask(s, src):
                sp.dma_start(maskb[:, s], src.rearrange("(t p) n -> p t n", p=P)).then_inc(mask_in[s], 16)

            def gat(base, layer, src, off):
                sp.dma_start(biasf[:, 0, :], gat_bias[layer]).then_inc(w_in, 16)
                load_mask(0, adj_t[0])
                load_mask(1, adj_t[1])

                def next_x(i, k, s):
                    sp.wait_ge(skip_ready, i + 1)
                    met(sp)
                    sp.dma_start(xin[:, s], nodes(src[k + 2])).then_inc(x_in[s], 16)

                def next_mask(i, k, s):
                    sp.wait_ge(wts_ready, i * H + H)
                    met(sp)
                    load_mask(s, adj_t[k + 2])

                def store(i, k):
                    sp.wait_ge(res_ready, i + 2)
                    met(sp)
                    sp.dma_start(nodes(out[k]), res[:, :, :]).then_inc(stored, 16)

                next_x(base, 0, 0)
                with sp.Fori(0, B // 2 - 2) as j:
                    for s in range(2):
                        k = j * 2 + s
                        next_mask(base + k, k, s)
                        next_x(base + k + 1, k + 1, 1 - s)
                        store(base + k, k)
                for k in range(B - 4, B):
                    if k + 2 < B:
                        next_mask(base + k, k, k % 2)
                    if k + 3 < B:
                        next_x(base + k + 1, k + 1, 1 - k % 2)
                    store(base + k, k)

            def mha(src, before):
                sp.dma_start(biasf[:, 0, 0:D], mha_bf).then_inc(m_bf_in, 16)
                load_mask(0, adj[0])
                load_mask(1, adj[1])
                first_graphs_stored(sp, before, B)
                sp.dma_start(res[:, :, :], nodes(src[0])).then_inc(m_x_in, 16)

                def turn(i, s, more):
                    if more:
                        sp.wait_ge(m_hn_ready, i + 1)
                        met(sp)
                        sp.dma_start(xin[:, s], nodes(src[i + 2])).then_inc(x_in[s], 16)
                        sp.wait_ge(m_negm_ready, i + 1)
                        met(sp)
                        load_mask(s, adj[i + 2])
                    sp.wait_ge(m_out_read, i * NT + NT + 1)
                    met(sp)
                    sp.dma_start(nodes(out[i]), res[:, :, :]).then_inc(stored, 16)

                def next_x(i):
                    sp.wait_ge(stored, (i + before) * 16 + 17)
                    met(sp)
                    sp.dma_start(res[:, :, :], nodes(src[i + 1])).then_inc(m_x_in, 16)

                with sp.Fori(0, B // 2 - 1) as j:
                    for s in range(2):
                        turn(j * 2 + s, s, True)
                        next_x(j * 2 + s)
                turn(B - 2, 0, False)
                next_x(B - 2)
                turn(B - 1, 1, False)

            walk(sp, gat, mha)
            total = {"g0": B, "g2": 2 * B, "m": B}
            sp.wait_ge(stored, 16 * sum(total[q] for q in passes) + 1)

        @block.tensor
        def _(pe):
            pe.wait_ge(const_done, 1)
            pe.sem_inc(back_done, 1)
            pe.sem_inc(m_pv_done, 1)
            pe.sem_inc(m_out_done, 1)

            def task(i, s, k):
                bank = ring[(s * TASKS + k) % 2]
                if not (isinstance(i, int) and i == 0 and k < 2):
                    pe.wait_ge(task_free, i * TASKS + k - 1)
                if k < T_H:
                    if k == 0:
                        pe.wait_ge(hn_ready, i + 1)
                    for t in range(NT):
                        last = nc.tensor.transpose(bank[:, t * P:(t + 1) * P], hn[:, t, k * P:(k + 1) * P], ident[:, :])
                elif k < T_HT[0] or k in T_Z:
                    is_h = k < T_HT[0]
                    t = k - T_H if is_h else T_Z.index(k)
                    cols = slice(0, D) if is_h else slice(D, 2 * D)
                    if k == T_H:
                        pe.wait_ge(task_free, i * TASKS + T_H)
                    nc.tensor.matmul(bank[:, 0:D], onesb[:, :], brow[:, cols], start=True, stop=False)
                    for c in range(KC):
                        last = nc.tensor.matmul(bank[:, 0:D], hnT[:, c, t * P:(t + 1) * P], wcat[:, c, cols],
                                                start=False, stop=c == KC - 1)
                elif k in T_HT:
                    c = T_HT.index(k)
                    if c == 0:
                        pe.wait_ge(task_free, i * TASKS + k)
                    for t in range(NT):
                        last = nc.tensor.transpose(bank[:, t * P:(t + 1) * P], hb[:, t, c * P:(c + 1) * P], ident[:, :])
                elif k in (T_D, T_S):
                    if k == T_D:
                        pe.wait_ge(task_free, i * TASKS + k)
                    for c in range(KC):
                        last = nc.tensor.matmul(bank[32 * c:32 * c + 32, :], wsd[:, c, int(k == T_D), :], thT[:, c, :],
                                                start=True, stop=True, tile_position=(0, 32 * c))
                else:
                    pe.wait_ge(task_free, i * TASKS + T_D + 1)
                    for t in range(NT):
                        last = nc.tensor.transpose(bank[:, t * P:(t + 1) * P], rows[:, t * P:(t + 1) * P], ident[:, :])
                last.then_inc(task_done, 1)

            def broadcast_v(i, s, a):
                if a == 0:
                    pe.wait_ge(vlo_ready, i + 1)
                if not (isinstance(i, int) and i == 0 and a < 4):
                    pe.wait_ge(wts_ready, i * H + a - 3)
                nc.tensor.matmul(vbc[a % 4][:, :], sel[:, a, :], vparts[:, s, :], start=True, stop=True).then_inc(vbc_done, 1)

            def weighted_sums(i, s, p):
                pe.wait_ge(vals_ready, i + 1)
                pe.wait_ge(wts_ready, i * H + 2 * p + 2)
                if not (isinstance(i, int) and i == 0 and p < 1):
                    pe.wait_ge(acc_free, i * PAIRS + p + 1)
                for t in range(NT):
                    for a in range(2):
                        last = nc.tensor.matmul(acc[64 * a:64 * a + 64, :], vals[:, s, t, 2 * p + a, :],
                                                wts[:, p % 2, a, t, :], start=t == 0, stop=t == NT - 1,
                                                tile_position=(0, 64 * a))
                last.then_inc(acc_done, 1)

            def turn_back(i, p):
                pe.wait_ge(acc_free, i * PAIRS + p + 2)
                if not (isinstance(i, int) and i == 0 and p < 1):
                    pe.wait_ge(o1_ready, i * PAIRS + p + 1)
                for t in range(NT):
                    last = nc.tensor.transpose(back[:, t * P:(t + 1) * P], accT[:, p % 2, t * P:(t + 1) * P], ident[:, :])
                last.then_inc(back_done, 1)

            def gat(base, layer, src, off):
                def pre(i, s):
                    for k in range(TASKS):
                        if k == T_H:
                            pe.wait_ge(w_in, 64 * (layer + 1))
                            pe.wait_ge(bias_done, layer + 1)
                        if k == T_D:
                            pe.wait_ge(wprep_pool, layer + 1)
                            pe.wait_ge(sel_ready, 1)
                        if k == TASKS - 1:
                            broadcast_v(i, s, 0)
                            broadcast_v(i, s, 1)
                        task(i, s, k)

                def slot(i, s, p, prev, nxt):
                    if p >= 1:
                        weighted_sums(i, s, p - 1)
                    elif prev:
                        weighted_sums(i - 1, 1 - s, PAIRS - 1)
                    if p < PAIRS - 1:
                        broadcast_v(i, s, 2 * p + 2)
                        broadcast_v(i, s, 2 * p + 3)
                    for n, k in enumerate(SLOT_TASKS[p]):
                        if nxt:
                            task(i + 1, 1 - s, k)
                        if n == 0 and p == PAIRS - 1 and nxt:
                            broadcast_v(i + 1, 1 - s, 0)
                            broadcast_v(i + 1, 1 - s, 1)
                        if n == 0 and p >= 1:
                            turn_back(i, p - 1)
                        elif n == 0 and prev:
                            turn_back(i - 1, PAIRS - 1)

                def drain(i, s):
                    weighted_sums(i, s, PAIRS - 1)
                    turn_back(i, PAIRS - 1)

                gat_slots(pe, base, pre, slot, drain)

            def mha(src, before):
                def mtask(i, s, n):
                    kind, c = MTASKS[n]
                    bank = mring[n % 2]
                    if not (isinstance(i, int) and i == 0 and n < 2):
                        pe.wait_ge(m_task_free, i * MT + (n - 1 if n >= 2 else 0))
                        if n < 2:
                            pe.wait_ge(m_split, i * len(SPLIT))
                        elif n - 2 in SPLIT:
                            pe.wait_ge(m_split, i * len(SPLIT) + SPLIT.index(n - 2) + 1)
                    if kind == "hT":
                        if c == 0:
                            pe.wait_ge(m_hn_ready, i + 1)
                        for t in range(NT):
                            last = nc.tensor.transpose(bank[:, t * P:(t + 1) * P], hn[:, t, c * P:(c + 1) * P], ident[:, :])
                    elif kind == "v":
                        for k in range(KC):
                            last = nc.tensor.matmul(bank[:, 0:D], hnT[:, k, c * P:(c + 1) * P], mwv[:, k, :],
                                                    start=k == 0, stop=k == KC - 1)
                    else:
                        w = mwq if kind == "q" else mwk
                        if n == SPLIT[0]:
                            pe.wait_ge(m_task_free, i * MT + KC)
                        for k in range(KC):
                            last = nc.tensor.matmul(bank[:, :], w[:, k, c * P:(c + 1) * P], hnT[:, k, :],
                                                    start=k == 0, stop=k == KC - 1)
                    last.then_inc(m_task_done, 1)

                def score(i, u):
                    h, t = u // NT, u % NT
                    if u % 8 == 0:
                        pe.wait_ge(m_split, i * len(SPLIT) + 2 * (h // 2) + 2)
                        pe.wait_ge(m_k_doubled, i * MPAIRS + h // 2 + 1)
                    if not (isinstance(i, int) and i == 0 and u < 2):
                        pe.wait_ge(m_masked, i * UNITS + u - 1)
                    for part in range(2):
                        last = nc.tensor.matmul(s_ps[u % 2][:, :], q_parts[:, h, t * P:(t + 1) * P], k_parts[:, part, h, :],
                                                start=part == 0, stop=part == 1)
                    last.then_inc(m_score_done, 1)

                def turn_probs(i, u):
                    pe.wait_ge(m_prob_ready, i * UNITS + u + 1)
                    if not (isinstance(i, int) and i == 0 and u < 2):
                        pe.wait_ge(m_probT_ready, i * UNITS + u - 1)
                    for k in range(NT):
                        last = nc.tensor.transpose(pt_ps[u % 2][:, k * P:(k + 1) * P], probs[:, u % 3, k * P:(k + 1) * P], ident[:, :])
                    last.then_inc(m_turned, 1)

                def context(i, s, q):
                    pe.wait_ge(m_probT_ready, i * UNITS + 8 * q + 8)
                    if q == 0:
                        pe.wait_ge(m_task_free, i * MT + MTASKS.index(("v", NT - 1)) + 1)
                    pe.wait_ge(m_ctx_ready, i * MPAIRS + q + 1)
                    for k in range(NT):
                        for a in range(2):
                            h = 2 * q + a
                            last = nc.tensor.matmul(ctx_ps[64 * a:64 * a + 64, :], mv_tile[:, s, k, h * MD:(h + 1) * MD],
                                                    probT[:, (s + q) % 2, a, k, :], start=k == 0, stop=k == NT - 1,
                                                    tile_position=(0, 64 * a))
                    last.then_inc(m_pv_done, 1)

                def project(i, t):
                    if t == 0:
                        pe.wait_ge(m_bias_done, 1)
                        pe.wait_ge(m_ctx_ready, i * MPAIRS + MPAIRS + 1)
                    pe.wait_ge(m_out_read, i * NT + t + 1)
                    nc.tensor.matmul(out_ps[:, 0:D], onesb[:, :], brow[:, 0:D], start=True, stop=False)
                    for c in range(KC):
                        last = nc.tensor.matmul(out_ps[:, 0:D], ctxT[:, c, t * P:(t + 1) * P], mwf[:, c, :],
                                                start=False, stop=c == KC - 1)
                    last.then_inc(m_out_done, 1)

                def pre(i, s):
                    for n in range(M_FIRST):
                        if n == SPLIT[0]:
                            pe.wait_ge(m_scaled, 1)
                        mtask(i, s, n)
                    score(i, 0)

                def at(i, s, u, prev, nxt):
                    if u < UNITS - 1:
                        score(i, u + 1)
                    elif nxt:
                        score(i + 1, 0)
                    if nxt and u in TASK_AT:
                        mtask(i + 1, 1 - s, TASK_AT[u])
                    if prev and u in LATE_AT:
                        mtask(i, s, LATE_AT[u])
                    if not prev and u + M_FIRST < MT:
                        mtask(i, s, M_FIRST + u)
                    if prev and u in OUT_AT:
                        project(i - 1, OUT_AT[u])
                    if u >= TURN:
                        turn_probs(i, u - TURN)
                    elif prev:
                        turn_probs(i - 1, u - TURN + UNITS)
                    if u >= AT_PV and (u - AT_PV) % 8 == 0:
                        context(i, s, (u - AT_PV) // 8)
                    elif prev and (u + UNITS - AT_PV) // 8 == 2 and (u + UNITS - AT_PV) % 8 == 0:
                        context(i - 1, 1 - s, 2)

                def drain(i, s):
                    for u in range(UNITS - TURN, UNITS):
                        turn_probs(i, u)
                    context(i, s, 2)
                    for t in range(NT):
                        project(i, t)

                mha_units(pe, pre, at, drain)

            walk(pe, gat, mha)

        @block.scalar
        def _(act):
            act.sem_inc(acc_free, 1)
            act.sem_inc(m_ctx_ready, 1)
            def load_first_graph(src, graphs, gat_graphs):
                if not isinstance(gat_graphs, int) or gat_graphs > 0:
                    act.wait_ge(skip_ready, gat_graphs)
                first_graphs_stored(act, graphs, 2)
                met(act)
                act.dma_start(xin[:, 0], nodes(src[0])).then_inc(x_in[0], 16)

            def load_second_graph(src):
                act.dma_start(xin[:, 1], nodes(src[1])).then_inc(x_in[1], 16)

            def normalize(i, s):
                act.wait_ge(nmr_ready, i + 1)
                act.wait_ge(hn_used, i) if not (isinstance(i, int) and i == 0) else None
                for t in range(NT):
                    last = nc.scalar.activation(hn[:, t, :], xin[:, s, t, :], ACT.Relu, bias=nmr[:, t:t + 1], scale=rstd[:, t:t + 1])
                last.then_inc(hn_ready, 1)

            def empty(i, s, k):
                bank = ring[(s * TASKS + k) % 2]
                act.wait_ge(task_done, i * TASKS + k + 1)
                if k < T_H:
                    last = nc.scalar.activation(hnT[:, k, :], bank[:, :], ACT.Copy)
                elif k < T_HT[0]:
                    if k == T_H and not (isinstance(i, int) and i == 0):
                        act.wait_ge(vals_ready, i)
                    last = nc.scalar.activation(hb[:, k - T_H, :], bank[:, 0:D], ACT.Copy)
                elif k in T_Z:
                    if k == T_Z[0] and not (isinstance(i, int) and i == 0):
                        act.wait_ge(res_ready, i)
                    last = nc.scalar.activation(gate[:, s, T_Z.index(k), :], bank[:, 0:D], ACT.Tanh, scale=0.5)
                elif k in T_HT:
                    last = nc.scalar.activation(thT[:, T_HT.index(k), :], bank[:, :], ACT.Tanh, bias=nb1[:, :])
                elif k == T_D:
                    act.wait_ge(dmax_ready, i + 1)
                    last = nc.scalar.activation(rows[0:ROWS, :], bank[0:ROWS, :], ACT.Exp, bias=dm[0:ROWS, 1:2],
                                                scale=slope[0:ROWS, 0:1])
                elif k == T_S:
                    last = nc.scalar.activation(vrow[0:ROWS, :], bank[0:ROWS, :], ACT.Relu, bias=dm[0:ROWS, 0:1])
                else:
                    by_head = bank.rearrange("p (t c r) -> p t c r", t=NT, c=4)
                    for tile, r in ((ucol[:, s, :, :], 0), (dcol[:, :, :], HC), (vals[:, s, :, :, E], HC)):
                        last = nc.scalar.activation(tile.rearrange("p t (c r) -> p t c r", c=KC),
                                                    by_head[:, :, 0:KC, r:r + HC], ACT.Copy)
                last.then_inc(task_free, 1)
                if k == T_S:
                    act.wait_ge(task_free, i * TASKS + T_S + 1)
                    nc.scalar.activation(vrow[0:ROWS, :], vrow[0:ROWS, :], ACT.Exp, scale=-0.8).then_inc(rows_ready, 1)
                    act.wait_ge(rows_ready, i + 1)
                    nc.scalar.activation(vparts[0:ROWS, s, :], vrow[0:ROWS, :], ACT.Copy).then_inc(vhi_ready, 1)

            def copy_acc(i, p):
                act.wait_ge(acc_done, i * PAIRS + p + 1)
                if not (isinstance(i, int) and i == 0 and p < 2):
                    act.wait_ge(back_done, i * PAIRS + p)
                nc.scalar.activation(accT[:, p % 2, :], acc[:, :], ACT.Copy).then_inc(acc_free, 1)

            def exps(i, s):
                act.wait_ge(o1_ready, i * PAIRS + PAIRS + 1)
                if not (isinstance(i, int) and i == 0):
                    act.wait_ge(res_ready, i + 1)
                nc.scalar.activation(ex[:, :, :], o1[:, s, :, :], ACT.Exp, bias=minus1[:, :]).then_inc(exp_done, 1)

            def gat(base, layer, src, off):
                load_first_graph(src, base + off, base)
                act.dma_start(wcat[:, :, :], gat_w[layer].rearrange("(c p) n -> p c n", p=P)).then_inc(w_in, 16)
                act.dma_start(wcol[:, :, :], gat_ws[layer].rearrange("(c p) s -> p c s", p=P)).then_inc(w_in, 16)
                act.dma_start(nb1[:, :], gat_bias[layer, 0, 0:P].rearrange("(p o) -> p o", o=1)).then_inc(w_in, 16)
                load_second_graph(src)

                def pre(i, s):
                    if isinstance(i, int) and i == 0:
                        act.wait_ge(const_done, 1)
                        nc.scalar.activation(sel[:, :, :], selF, ACT.Copy).then_inc(sel_ready, 1)
                    normalize(i, s)
                    for k in range(TASKS):
                        if k == T_HT[0]:
                            act.wait_ge(bias_done, layer + 1)
                        if k == T_D:
                            normalize(i + 1, 1 - s)
                            act.wait_ge(vals_cleared, layer + 1)
                        empty(i, s, k)

                def slot(i, s, p, prev, nxt):
                    if p == 2 and prev:
                        exps(i - 1, 1 - s)
                    if p >= 1:
                        copy_acc(i, p - 1)
                    elif prev:
                        copy_acc(i - 1, PAIRS - 1)
                    if nxt:
                        for k in SLOT_TASKS[p]:
                            empty(i + 1, 1 - s, k)
                    if nxt == 2 and p == 5:
                        normalize(i + 2, s)

                def drain(i, s):
                    copy_acc(i, PAIRS - 1)
                    exps(i, s)

                gat_slots(act, base, pre, slot, drain)

            def mha(src, before):
                load_first_graph(src, before, before)
                if before:
                    act.wait_ge(vals_ready, before)
                for tile, w in ((mwq, wq), (mwk, wk), (mwv, wv), (mwf[:, :, :], wf)):
                    act.dma_start(tile, w.rearrange("(c p) n -> p c n", p=P)).then_inc(m_w_in, 16)
                act.dma_start(mbias[:, :, :], mha_bias).then_inc(m_w_in, 16)
                load_second_graph(src)

                def normalize(i, s, tiles=range(NT)):
                    act.wait_ge(m_nmr_ready, i + 1)
                    for t in tiles:
                        last = nc.scalar.activation(hn[:, t, :], xin[:, s, t, :], ACT.Relu, bias=nmr[:, t:t + 1], scale=rstd[:, t:t + 1])
                    if tiles[-1] == NT - 1:
                        last.then_inc(m_hn_ready, 1)

                def empty(i, s, n):
                    kind, c = MTASKS[n]
                    bank = mring[n % 2]
                    act.wait_ge(m_task_done, i * MT + n + 1)
                    if kind == "hT":
                        last = nc.scalar.activation(hnT[:, c, :], bank[:, :], ACT.Copy)
                    elif kind == "v":
                        last = nc.scalar.activation(mv_tile[:, s, c, :], bank[:, 0:D], ACT.Copy)
                    else:
                        for a in range(2):
                            own = slice(64 * a, 64 * a + 64)
                            if kind == "q":
                                last = nc.scalar.activation(q_parts[own, 2 * c + a, :], bank[own, :], ACT.Identity,
                                                            bias=mbias[own, 0, c:c + 1])
                            else:
                                for to in (slice(0, 64), slice(64, P)):
                                    last = nc.scalar.activation(k_parts[to, 0, 2 * c + a, :], bank[own, :], ACT.Identity,
                                                                bias=mbias[own, 1, c:c + 1])
                    last.then_inc(m_task_free, 1)

                def double_low(i, n):
                    c = MTASKS[n][1]
                    act.wait_ge(m_split, i * len(SPLIT) + SPLIT.index(n) + 1)
                    for a in range(2):
                        own, other = slice(64 * a, 64 * a + 64), slice(64 * (1 - a), 64 * (1 - a) + 64)
                        last = nc.scalar.activation(k_parts[other, 1, 2 * c + a, :],
                                                    k_parts[own, 1, 2 * c + a, :].bitcast(F32), ACT.Copy)
                    last.then_inc(m_k_doubled, 1)

                def exp(i, u):
                    act.wait_ge(m_masked, i * UNITS + u + 1)
                    if not (isinstance(i, int) and i == 0 and u < 3):
                        act.wait_ge(m_prob_ready, i * UNITS + u - 2)
                    r = u % 3
                    nc.scalar.activation(expd[:, r, :], scores[:, r, :], ACT.Exp, bias=nmax[:, r:r + 1], scale=-1.0,
                                         accum_out=rsum[:, r:r + 1]).then_inc(m_exp_done, 1)

                def copy_ctx(i, q):
                    act.wait_ge(m_pv_done, i * MPAIRS + q + 2)
                    if q == 0:
                        act.wait_ge(m_out_done, i * NT + 1)
                    nc.scalar.activation(ctxT[:, q, :], ctx_ps[:, :], ACT.Identity, bias=mbias[:, 2, q:q + 1]).then_inc(m_ctx_ready, 1)

                def pre(i, s):
                    normalize(i, s)
                    for n in range(M_FIRST):
                        if n == SPLIT[0]:
                            act.wait_ge(m_scaled, 1)
                        empty(i, s, n)
                        if MTASKS[n][0] == "k":
                            double_low(i, n)

                def at(i, s, u, prev, nxt):
                    exp(i, u)
                    for due, n in tuple(TASK_AT.items()) + tuple(LATE_AT.items()):
                        if MTASKS[n][0] != "k" or (due + 3) % UNITS != u:
                            continue
                        if n in TASK_AT.values() and due + 3 < UNITS:
                            if nxt:
                                double_low(i + 1, n)
                        elif prev:
                            double_low(i, n)
                    if not prev and u >= 3 and M_FIRST + u - 3 < MT and MTASKS[M_FIRST + u - 3][0] == "k":
                        double_low(i, M_FIRST + u - 3)
                    if nxt and u == AT_STATS + 2:
                        normalize(i + 1, 1 - s, range(2))
                    if nxt and u == AT_STATS + 3:
                        normalize(i + 1, 1 - s, range(2, NT))
                    if nxt and u in TASK_AT:
                        empty(i + 1, 1 - s, TASK_AT[u])
                    if prev and u in LATE_AT:
                        empty(i, s, LATE_AT[u])
                    if not prev and u + M_FIRST < MT:
                        empty(i, s, M_FIRST + u)
                    if u >= AT_PV and (u - AT_PV) % 8 == 0:
                        copy_ctx(i, (u - AT_PV) // 8)
                    elif prev and u == AT_PV + 16 - UNITS:
                        copy_ctx(i - 1, 2)

                mha_units(act, pre, at, lambda i, s: copy_ctx(i, 2))

            walk(act, gat, mha)

        @block.vector
        def _(dve):
            dve.sem_inc(o1_ready, 1)
            dve.sem_inc(res_ready, 1)
            dve.sem_inc(m_out_read, 1)
            nc.vector.memset(rows[:, :], 0.0)
            nc.vector.memset(vparts[:, :, :].bitcast(F32), 0.0)
            nc.vector.memset(brow[:, :], 0.0)
            nc.vector.memset(onesb[:, :], 0.0)
            nc.vector.memset(slope[:, :], 0.2)
            nc.vector.memset(low[:, :], 0.0)
            nc.vector.memset(minus1[:, :], -1.0).then_inc(const_step, 1)
            dve.wait_ge(const_step, 1)
            for q in (Q0, Q1, Q2):
                nc.vector.memset(slope[q:q + HC, :], 0.8)
                nc.vector.memset(low[q:q + 2 * HC, :], -1.0)
            for q in (Q0, Q1):
                nc.vector.memset(onesb[q:q + 1, :], 1.0)
            nc.vector.memset(onesb[Q2:Q2 + 1, :], 1.0).then_inc(const_step, 1)
            dve.wait_ge(const_step, 2)
            for q in (Q0, Q1, Q2):
                last = nc.vector.memset(low[q:q + HC, :], 0.0)
            last.then_inc(const_step, 1)

            def ln_stats(s, loads, n, stats_done, aggr_done, var_done):
                dve.wait_ge(x_in[s], loads)
                for t in range(NT):
                    last = nc.vector.bn_stats(st6[:, t, :], xin[:, s, t, :])
                last.then_inc(stats_done, 1)
                dve.wait_ge(stats_done, n)
                met(dve)
                for t in range(NT):
                    last = nc.vector.bn_aggr(mv[:, t, :], st6[:, t, :])
                last.then_inc(aggr_done, 1)
                dve.wait_ge(aggr_done, n)
                nc.vector.tensor_scalar(veps[:, :], mv[:, :, 1], EPS, None, ALU.add).then_inc(var_done, 1)

            def bias_rows(layer):
                n = [layer * 6]

                def link(ins):
                    n[0] = n[0] + 1
                    ins.then_inc(bias_step, 1)
                    dve.wait_ge(bias_step, n[0])

                dve.wait_ge(w_in, 64 * (layer + 1))
                nc.vector.tensor_scalar(nb1[:, :], nb1[:, :], -1.0, -1.0, ALU.mult, ALU.add)
                link(nc.vector.tensor_scalar(biasf[:, 0, 0:D], biasf[:, 0, 0:D], 1.0, None, ALU.add))
                link(nc.vector.tensor_copy(brow[0:1, :], biasf[:, 0, :]))
                link(nc.vector.tensor_tensor(biasf[:, 1, :], biasf[:, 0, :], brow[0:1, :], ALU.subtract))
                link(nc.vector.tensor_copy(biasp[:, 0, :], biasf[:, 1, :]))
                link(nc.vector.tensor_tensor(biasf[:, 2, :], biasf[:, 1, :], biasp[:, 0, :], ALU.subtract))
                link(nc.vector.tensor_copy(brow[Q1:Q1 + 1, :], biasp[:, 0, :]))
                nc.vector.tensor_copy(brow[Q2:Q2 + 1, :], biasf[:, 2, :]).then_inc(bias_done, 1)

            def neg_mean(i):
                dve.wait_ge(rstd_ready, i + 1)
                nc.vector.scalar_tensor_tensor(out=nmr[:, :], in0=mv[:, :, 0], scalar=-1.0, in1=rstd[:, :],
                                               op0=ALU.mult, op1=ALU.mult).then_inc(nmr_ready, 1)

            def dmax(i, s):
                d_bank = ring[(s * TASKS + T_D) % 2]
                dve.wait_ge(task_done, i * TASKS + T_D + 1)
                nc.vector.tensor_reduce(dm[0:ROWS, 0:1], d_bank[0:ROWS, :], AX_X, ALU.max).then_inc(dmax_done, 1)
                dve.wait_ge(dmax_done, i + 1)
                nc.vector.scalar_tensor_tensor(out=dm[0:ROWS, 1:2], in0=dm[0:ROWS, 0:1], scalar=-1.0, in1=slope[0:ROWS, :],
                                               op0=ALU.mult, op1=ALU.mult).then_inc(dmax_ready, 1)

            def v_low(i, s):
                dve.wait_ge(vhi_ready, i + 1)
                nc.vector.scalar_tensor_tensor(out=vparts[0:ROWS, s, :], in0=vparts[0:ROWS, s, :].bitcast(F32),
                                               scalar=low[0:ROWS, :], in1=vrow[0:ROWS, :],
                                               op0=ALU.mult, op1=ALU.add).then_inc(vlo_ready, 1)

            def values(i, s):
                dve.wait_ge(task_free, i * TASKS + T_COL + 1)
                nc.vector.tensor_tensor(vals[:, s, :, :, 0:E], hb[:, :, :].rearrange("p t (a e) -> p t a e", e=E),
                                        dcol[:, :, :].unsqueeze(3).to_broadcast([P, NT, H, E]),
                                        ALU.mult).then_inc(vals_ready, 1)

            def weights(i, s, a):
                dve.wait_ge(vbc_done, i * H + a + 1)
                if a == 0:
                    dve.wait_ge(task_free, i * TASKS + T_COL + 1)
                if a % 2 == 0 and not (isinstance(i, int) and i == 0 and a < 4):
                    dve.wait_ge(acc_done, i * PAIRS + a // 2 - 1)
                for t in range(NT):
                    last = nc.vector.scalar_tensor_tensor(out=wts[:, a // 2 % 2, a % 2, t, :], in0=vbc[a % 4][:, :],
                                                          scalar=ucol[:, s, t, a:a + 1], in1=maskb[:, s, t, :],
                                                          op0=ALU.max, op1=ALU.mult)
                last.then_inc(wts_ready, 1)

            def divide(i, s, p):
                g = i * PAIRS + p + 1
                b4 = back.rearrange("p (t a c) -> p t a c", t=NT, a=2)
                dve.wait_ge(back_done, g + 1)
                nc.vector.reciprocal(rcp[:, :, :], b4[:, :, :, E]).then_inc(rcp_done, 1)
                dve.wait_ge(rcp_done, g)
                nc.vector.tensor_tensor(o1[:, s, :, 2 * p * E:(2 * p + 2) * E].rearrange("p t (a e) -> p t a e", e=E),
                                        b4[:, :, :, 0:E], rcp[:, :, :].unsqueeze(3).to_broadcast([P, NT, 2, E]),
                                        ALU.mult).then_inc(o1_ready, 1)

            def finish(i, s, off):
                dve.wait_ge(exp_done, i + 1)
                nc.vector.scalar_tensor_tensor(out=ex[:, :, :], in0=ex[:, :, :], scalar=1.0, in1=o1[:, s, :, :],
                                               op0=ALU.min, op1=ALU.max).then_inc(elu_done, 1)
                dve.wait_ge(elu_done, i + 1)
                dve.wait_ge(skip_ready, i + 1)
                nc.vector.tensor_tensor(ex[:, :, :], ex[:, :, :], gate[:, s, :, :], ALU.mult).then_inc(gated, 1)
                dve.wait_ge(gated, i + 1)
                dve.wait_ge(stored, (i + off) * 16 + 1)
                nc.vector.tensor_tensor(res[:, :, :], ex[:, :, :], skip[:, s, :, :], ALU.add).then_inc(res_ready, 1)

            def gat(base, layer, src, off):

                def nth(i, s):
                    return 8 * (i + off - s) + 16

                def pre(i, s):
                    stats(i, s)
                    neg_mean(i)
                    bias_rows(layer)
                    stats(i + 1, 1 - s)
                    neg_mean(i + 1)
                    dve.wait_ge(mask_in[s], nth(i, s))
                    dmax(i, s)
                    v_low(i, s)
                    values(i, s)

                def stats(i, s):
                    ln_stats(s, nth(i, s), i + 1, bn_stats_done, bn_aggr_done, var_ready)

                def slot(i, s, p, prev, nxt):
                    if p == 0 and prev:
                        dve.wait_ge(mask_in[s], nth(i, s))
                    weights(i, s, 2 * p)
                    if p == 0 and prev:
                        values(i, s)
                    if p >= 2:
                        divide(i, s, p - 2)
                    elif prev:
                        divide(i - 1, 1 - s, PAIRS + p - 2)
                    if p == 4 and nxt == 2:
                        neg_mean(i + 2)
                    if p == 5 and nxt:
                        v_low(i + 1, 1 - s)
                    weights(i, s, 2 * p + 1)
                    if p == 4 and nxt:
                        dmax(i + 1, 1 - s)
                    if p == 2 and prev:
                        finish(i - 1, 1 - s, off)
                    if p == 3 and nxt == 2:
                        stats(i + 2, s)

                def drain(i, s):
                    divide(i, s, PAIRS - 2)
                    divide(i, s, PAIRS - 1)
                    finish(i, s, off)

                gat_slots(dve, base, pre, slot, drain)

            def mha(src, before):
                def prepare_weights():
                    made = [0]

                    def link(ins):
                        made[0] += 1
                        ins.then_inc(m_bias_step, 1)
                        dve.wait_ge(m_bias_step, made[0])

                    dve.wait_ge(m_w_in, 16 * 5)
                    nc.vector.tensor_scalar(mwq, mwq, 0.125, None, ALU.mult)
                    nc.vector.tensor_scalar(mbias[:, 0, :], mbias[:, 0, :], 0.125, None, ALU.mult).then_inc(m_scaled, 1)
                    dve.wait_ge(m_bf_in, 16)
                    link(nc.vector.tensor_copy(brow[0:1, 0:D], biasf[:, 0, 0:D]))
                    link(nc.vector.tensor_tensor(biasf[:, 1, 0:D], biasf[:, 0, 0:D], brow[0:1, 0:D], ALU.subtract))
                    link(nc.vector.tensor_copy(biasp[:, 0, 0:D], biasf[:, 1, 0:D]))
                    link(nc.vector.tensor_tensor(biasf[:, 2, 0:D], biasf[:, 1, 0:D], biasp[:, 0, 0:D], ALU.subtract))
                    link(nc.vector.tensor_copy(brow[Q1:Q1 + 1, 0:D], biasp[:, 0, 0:D]))
                    nc.vector.tensor_copy(brow[Q2:Q2 + 1, 0:D], biasf[:, 2, 0:D]).then_inc(m_bias_done, 1)

                def stats(i, s):
                    ln_stats(s, 8 * (i + before - s) + 16, i + 1, m_stats_done, m_aggr_done, m_var_ready)

                def neg_mean(i):
                    dve.wait_ge(m_rstd_ready, i + 1)
                    nc.vector.scalar_tensor_tensor(out=nmr[:, :], in0=mv[:, :, 0], scalar=-1.0, in1=rstd[:, :],
                                                   op0=ALU.mult, op1=ALU.mult).then_inc(m_nmr_ready, 1)

                def split(i, n):
                    kind, c = MTASKS[n]
                    bank = mring[n % 2]
                    dve.wait_ge(m_task_free, i * MT + n + 1)
                    for a in range(2):
                        own, other = slice(64 * a, 64 * a + 64), slice(64 * (1 - a), 64 * (1 - a) + 64)
                        if kind == "q":
                            last = nc.vector.scalar_tensor_tensor(out=q_parts[other, 2 * c + a, :], in0=bank[own, :],
                                                                  scalar=mbias[own, 0, c:c + 1],
                                                                  in1=q_parts[own, 2 * c + a, :].bitcast(F32),
                                                                  op0=ALU.add, op1=ALU.subtract)
                        else:
                            last = nc.vector.scalar_tensor_tensor(out=k_parts[own, 1, 2 * c + a, :], in0=bank[own, :],
                                                                  scalar=mbias[own, 1, c:c + 1],
                                                                  in1=k_parts[own, 0, 2 * c + a, :].bitcast(F32),
                                                                  op0=ALU.add, op1=ALU.subtract)
                    last.then_inc(m_split, 1)

                def masked(i, s, u):
                    if u == 0:
                        dve.wait_ge(m_negm_ready, i + 1)
                    dve.wait_ge(m_score_done, i * UNITS + u + 1)
                    if not (isinstance(i, int) and i == 0 and u < 3):
                        dve.wait_ge(m_exp_done, i * UNITS + u - 2)
                    met(dve)
                    r = u % 3
                    nc.vector.tensor_tensor_reduce(out=scores[:, r, :], in0=s_ps[u % 2][:, :], in1=negm[:, s, u % NT, :],
                                                   scale=-1.0, scalar=3e38, op0=ALU.add, op1=ALU.min,
                                                   accum_out=nmax[:, r:r + 1]).then_inc(m_masked, 1)

                def invert(i, u):
                    dve.wait_ge(m_exp_done, i * UNITS + u + 1)
                    if not (isinstance(i, int) and i == 0 and u < 3):
                        dve.wait_ge(m_prob_ready, i * UNITS + u - 2)
                    nc.vector.reciprocal(rinv[:, u % 3:u % 3 + 1], rsum[:, u % 3:u % 3 + 1]).then_inc(m_rinv_ready, 1)

                def copy_probT(i, s, u):
                    h, t = u // NT, u % NT
                    q = h // 2
                    dve.wait_ge(m_turned, i * UNITS + u + 1)
                    if u % 8 == 0 and not (isinstance(i, int) and i == 0 and q < 2):
                        dve.wait_ge(m_pv_done, i * MPAIRS + q)
                    nc.vector.tensor_copy(probT[:, (s + q) % 2, h % 2, :, t * P:(t + 1) * P],
                                          pt_ps[u % 2].rearrange("p (k n) -> p k n", k=NT)).then_inc(m_probT_ready, 1)

                def residual(i, t):
                    dve.wait_ge(m_out_done, i * NT + t + 2)
                    if t == 0:
                        dve.wait_ge(m_x_in, i * 16 + 16)
                    nc.vector.tensor_tensor(res[:, t, :], out_ps[:, 0:D], res[:, t, :], ALU.add).then_inc(m_out_read, 1)

                def pre(i, s):
                    stats(i, s)
                    neg_mean(i)
                    prepare_weights()
                    for n in SPLIT:
                        if n < M_FIRST:
                            split(i, n)

                def at(i, s, u, prev, nxt):
                    masked(i, s, u)
                    if u >= 1:
                        invert(i, u - 1)
                    elif prev:
                        invert(i - 1, UNITS - 1)
                    if u > TURN:
                        copy_probT(i, s, u - TURN - 1)
                    elif prev:
                        copy_probT(i - 1, 1 - s, u - TURN - 1 + UNITS)
                    if prev and u in OUT_AT:
                        residual(i - 1, OUT_AT[u])
                    if nxt and TASK_AT.get(u - 2) in SPLIT:
                        split(i + 1, TASK_AT[u - 2])
                    if prev and TASK_AT.get(u - 2 + UNITS) in SPLIT:
                        split(i, TASK_AT[u - 2 + UNITS])
                    if prev and LATE_AT.get(u - 2) in SPLIT:
                        split(i, LATE_AT[u - 2])
                    if not prev and M_FIRST + u - 2 in SPLIT and u >= 2:
                        split(i, M_FIRST + u - 2)
                    if nxt and u == AT_STATS:
                        stats(i + 1, 1 - s)
                    if nxt and u == AT_STATS + 1:
                        neg_mean(i + 1)

                def drain(i, s):
                    invert(i, UNITS - 1)
                    for u in range(UNITS - TURN - 1, UNITS):
                        copy_probT(i, s, u)
                    for t in range(NT):
                        residual(i, t)

                mha_units(dve, pre, at, drain)

            walk(dve, gat, mha)

        @block.gpsimd
        def _(pool):
            made = [0]

            def link(ins):
                made[0] += 1
                ins.then_inc(pool_const, 1)
                pool.wait_ge(pool_const, made[0])

            link(nc.gpsimd.memset(ident[:, :], 0.0))
            link(nc.gpsimd.memset(selF, 0.0))
            link(nc.gpsimd.memset(wsd[:, :, :], 0.0))
            link(nc.gpsimd.memset(mhalf[:, :], -0.5))
            link(nc.gpsimd.affine_select(out=ident[:, :], in_=ident[:, :], compare_op=ALU.not_equal, fill=1.0,
                                         base=0, pattern=[[-1, P]], channel_multiplier=1))
            for first in (0, HC):
                by_row = selF.rearrange("p (c r) n -> p c r n", c=KC)
                link(nc.gpsimd.affine_select(out=by_row, in_=by_row, compare_op=ALU.not_equal, fill=1.0, base=-first,
                                             pattern=[[-32, KC], [-1, HC], [0, P]], channel_multiplier=1))
            pool.wait_ge(const_step, 3)
            pool.sem_inc(const_done, 1)

            def rsqrt(i):
                pool.wait_ge(var_ready, i + 1)
                nc.gpsimd.tensor_tensor(rstd[:, :], veps[:, :], mhalf[:, :], ALU.pow).then_inc(rstd_ready, 1)

            def skip_early(i, s):
                pool.wait_ge(hn_ready, i + 1)
                if not (isinstance(i, int) and i == 0):
                    pool.wait_ge(res_ready, i)
                nc.gpsimd.tensor_tensor(skip[:, s, :, :], xin[:, s, :, :], hn[:, :, :], ALU.add).then_inc(xh_done, 1)
                if not (isinstance(i, int) and i == 0):
                    pool.wait_ge(skip_ready, i)
                    met(pool)
                nc.gpsimd.tensor_scalar(hn1[:, :, :], hn[:, :, :], 1.0, 1.0, ALU.add, ALU.mult).then_inc(hn_used, 1)

            def skip_late(i, s):
                pool.wait_ge(task_free, i * TASKS + T_Z[-1] + 1)
                pool.wait_ge(hn_used, i + 1)
                met(pool)
                nc.gpsimd.tensor_scalar(gate[:, s, :, :], gate[:, s, :, :], 0.5, 0.5, ALU.mult, ALU.add).then_inc(gate_half, 1)
                pool.wait_ge(gate_half, i + 1)
                nc.gpsimd.tensor_tensor(hn1[:, :, :], hn1[:, :, :], gate[:, s, :, :], ALU.mult).then_inc(gate_prod, 1)
                pool.wait_ge(gate_prod, i + 1)
                pool.wait_ge(xh_done, i + 1)
                nc.gpsimd.tensor_tensor(skip[:, s, :, :], skip[:, s, :, :], hn1[:, :, :], ALU.subtract).then_inc(skip_ready, 1)

            def gat(base, layer, src, off):
                def pre(i, s):
                    rsqrt(i)
                    pool.wait_ge(rstd_ready, i + 1)
                    pool.wait_ge(w_in, 64 * (layer + 1))
                    met(pool)
                    for j in range(HC):
                        own = slice(E * j, E * j + E)
                        for first in (0, HC):
                            last = nc.gpsimd.tensor_copy(wsd[own, :, :, first + j], wcol[own, :, :])
                    last.then_inc(wprep_pool, 1)
                    pool.wait_ge(wprep_pool, layer + 1)
                    pool.wait_ge(hn_ready, i + 1)
                    rsqrt(i + 1)
                    skip_early(i, s)
                    nc.gpsimd.memset(vals[:, :, :, :, :], 0.0).then_inc(vals_cleared, 1)

                def slot(i, s, p, prev, nxt):
                    if p == 3 and nxt == 2:
                        rsqrt(i + 2)
                    if p == 0:
                        skip_late(i, s)
                    if p == 1 and nxt:
                        skip_early(i + 1, 1 - s)

                gat_slots(pool, base, pre, slot, lambda i, s: None)

            def mha(src, before):
                def rsqrt(i):
                    pool.wait_ge(m_var_ready, i + 1)
                    nc.gpsimd.tensor_tensor(rstd[:, :], veps[:, :], mhalf[:, :], ALU.pow).then_inc(m_rstd_ready, 1)

                def mask(i, s):
                    pool.wait_ge(mask_in[s], 8 * (i + before - s) + 16)
                    met(pool)
                    nc.gpsimd.tensor_scalar(negm[:, s, :, :], maskb[:, s, :, :], -1.0, -NEG, ALU.add, ALU.mult).then_inc(m_negm_ready, 1)

                def scale(i, u):
                    r = u % 3
                    pool.wait_ge(m_rinv_ready, i * UNITS + u + 1)
                    if not (isinstance(i, int) and i == 0 and u < 3):
                        pool.wait_ge(m_turned, i * UNITS + u - 2)
                    met(pool)
                    nc.gpsimd.tensor_scalar(probs[:, r, :], expd[:, r, :], rinv[:, r:r + 1], 1.0, ALU.mult, ALU.mult).then_inc(m_prob_ready, 1)

                def pre(i, s):
                    rsqrt(i)
                    mask(i, s)

                def at(i, s, u, prev, nxt):
                    if u >= 1:
                        scale(i, u - 1)
                    elif prev:
                        scale(i - 1, UNITS - 1)
                    if nxt and u == AT_STATS:
                        rsqrt(i + 1)
                    if nxt and u == AT_PV + 1:
                        mask(i + 1, 1 - s)

                mha_units(pool, pre, at, lambda i, s: scale(i, UNITS - 1))

            walk(pool, gat, mha)


def layout(inputs):
    import numpy as np

    def a(name):
        return np.asarray(inputs[name])

    gat = ("L0_gnn_", "L2_gnn_", "L3_gnn_")
    adj = a("adj")
    return {
        "x": np.ascontiguousarray(a("x")),
        "adj": np.ascontiguousarray(adj),
        "adj_t": np.ascontiguousarray(adj.transpose(0, 2, 1)),
        "gat_w": np.stack([np.concatenate([a(g + "W").transpose(1, 0, 2).reshape(D, D), a(g + "H_w").T], 1) for g in gat]),
        "gat_bias": np.stack([np.concatenate([np.tile(a(g + "b"), H), a(g + "H_b")])[None] for g in gat]),
        "gat_ws": np.stack([np.stack([a(g + "w_src").reshape(D), a(g + "w_dst").reshape(D)], 1) for g in gat]),
        "wq": a("L1_gnn_Wq"), "wk": a("L1_gnn_Wk"), "wv": a("L1_gnn_Wv"), "wf": a("L1_gnn_Wf"),
        "mha_bias": np.ascontiguousarray(np.stack([a("L1_gnn_" + n) for n in ("bq", "bk", "bv")]).reshape(3, KC, P).transpose(2, 0, 1)),
        "mha_bf": a("L1_gnn_bf")[None],
    }


def kernel(**inputs):
    import numpy as np
    import concourse.bacc as bacc
    from concourse import mybir as mb
    from concourse.bass_utils import run_bass_kernel_spmd

    arrays = layout(inputs)
    nc = bacc.Bacc("TRN2", target_bir_lowering=False, num_devices=1)
    aps = [nc.dram_tensor(n, v.shape, mb.dt.from_np(v.dtype), kind="ExternalInput").ap() for n, v in arrays.items()]
    out = nc.dram_tensor("out", (B, N, D), mb.dt.float32, kind="ExternalOutput").ap()
    program(nc, *aps, out)
    r = run_bass_kernel_spmd(nc, [arrays], core_ids=[0])
    return np.asarray(r.results[0]["out"])
```
